# Optimizing a Trainium2 kernel written in Bass

```python
import numpy as np
import jax
import jax.numpy as jnp

def _softmax(x, axis=-1):
    return jax.nn.softmax(x, axis=axis)

def _gelu(x):
    return jax.nn.gelu(x, approximate=True)

def _silu(x):
    return jax.nn.silu(x)

def _sigmoid(x):
    return jax.nn.sigmoid(x)

def _layernorm(x, axis=-1, eps=1e-05):
    m = jnp.mean(x, axis=axis, keepdims=True)
    v = jnp.var(x, axis=axis, keepdims=True)
    return (x - m) / jnp.sqrt(v + eps)

def _scatter_add(tgt, idx, src, axis=0):
    return tgt.at[idx].add(src)

def _segment_sum(src, seg, n):
    return jax.ops.segment_sum(src, seg, n)
kernel_name = 'mk_vit_tower_cls_d1_tok_img256_r4_5b6f8b'

def setup_inputs(seed: int=0):
    np.random.seed(seed)
    _w = jnp.asarray

    def _rec_inputs():
        import jax
        import jax.numpy as jnp
        _rk = jax.random.key(seed)
        x = -7.10856e-05 + 0.999911 * jax.random.normal(jax.random.fold_in(_rk, 1), (64, 1, 112, 112), jnp.float32)
        cls_tok = 0.02 * jax.random.normal(jax.random.fold_in(_rk, 5), (1, 1, 64), jnp.float32)
        return (x, cls_tok)
    x, cls_tok = _rec_inputs()

    def _L0_tok_setup():
        import jax, jax.numpy as jnp
        import numpy as np
        INV_SQRT2 = 0.7071067811865476

        def haar_dwt2(x):
            lo = (x[..., ::2] + x[..., 1::2]) * INV_SQRT2
            hi = (x[..., ::2] - x[..., 1::2]) * INV_SQRT2
            cA = (lo[..., ::2, :] + lo[..., 1::2, :]) * INV_SQRT2
            cH = (lo[..., ::2, :] - lo[..., 1::2, :]) * INV_SQRT2
            cV = (hi[..., ::2, :] + hi[..., 1::2, :]) * INV_SQRT2
            cD = (hi[..., ::2, :] - hi[..., 1::2, :]) * INV_SQRT2
            return (cA, (cH, cV, cD))

        def wavedec2_maps(x, levels):
            a = x
            details = []
            for _ in range(levels):
                a, d = haar_dwt2(a)
                details.append(d)
            maps = [a]
            for d in reversed(details):
                maps.extend(d)
            return maps
        key = jax.random.key(seed)
        k1, k2 = jax.random.split(key)
        B, H, W_img = (64, 256, 256)
        x = jax.random.normal(k1, (B, 1, H, W_img), dtype=jnp.float32)
        n_maps = 1 + 3 * 2
        W = jax.random.normal(k2, (n_maps, 64), dtype=jnp.float32) * (1.0 / np.sqrt(n_maps))
        b = jnp.zeros((64,), dtype=jnp.float32)
        return {'x': x, 'W': W, 'b': b}
    _L0_tok_all = _L0_tok_setup()
    _L0_tok_in = {k: v for k, v in _L0_tok_all.items() if k in ('W', 'b')}
    del _L0_tok_all

    def _L0_attn_setup():
        import jax, jax.numpy as jnp
        import numpy as np
        import math
        B, L, C = (1024, 64, 64)
        H = 8
        META_H = 96

        def _rel_coords_log(W):
            c0 = jnp.zeros((W,), jnp.float32)
            c1 = jnp.arange(W, dtype=jnp.float32)
            coords = jnp.stack([c0, c1], axis=0)
            rel = coords[:, :, None] - coords[:, None, :]
            rel = rel.transpose(1, 2, 0).reshape(-1, 2)
            return jnp.sign(rel) * jnp.log1p(jnp.abs(rel))
        key = jax.random.key(seed)
        ks = jax.random.split(key, 8)
        s = 0.02
        return {'x': jax.random.normal(ks[0], (B, L, C), jnp.float32), 'qkv_w': jax.random.normal(ks[1], (3 * C, C), jnp.float32) * s, 'qkv_b': jnp.zeros((3 * C,), jnp.float32), 'proj_w': jax.random.normal(ks[2], (C, C), jnp.float32) * s, 'proj_b': jnp.zeros((C,), jnp.float32), 'logit_scale': jnp.full((H,), math.log(10.0), jnp.float32), 'mlp1_w': jax.random.normal(ks[3], (META_H, 2), jnp.float32) * s, 'mlp1_b': jnp.zeros((META_H,), jnp.float32), 'mlp2_w': jax.random.normal(ks[4], (H, META_H), jnp.float32) * s, 'mlp2_b': jnp.zeros((H,), jnp.float32)}
    _L0_attn_all = _L0_attn_setup()
    _L0_attn_in = {k: v for k, v in _L0_attn_all.items() if k in ('qkv_w', 'qkv_b', 'proj_w', 'proj_b', 'logit_scale', 'mlp1_w', 'mlp1_b', 'mlp2_w', 'mlp2_b')}
    del _L0_attn_all

    def _L0_ffn_setup():
        import jax, jax.numpy as jnp
        import numpy as np
        DIM = 64
        HEADS = 8
        NUM_KEYS = 64
        NUM_KV = NUM_KEYS ** 2
        PK_TOPK = 16
        FINAL_TOPK = 16
        DIM_KEY = DIM // 2
        P = 2

        def _pk(x, Wq_pk, pk_keys):
            b, n, _ = x.shape
            q = (x @ Wq_pk).reshape(b, n, P, HEADS, DIM_KEY).transpose(2, 0, 1, 3, 4)
            sim = jnp.einsum('pbnhd,pkhd->pbnhk', q, pk_keys)
            scores, idx = jax.lax.top_k(sim, PK_TOPK)
            idx0 = idx[0]
            idx1 = idx[1] * NUM_KEYS
            index = (idx0[..., :, None] + idx1[..., None, :]).reshape(b, n, HEADS, PK_TOPK * PK_TOPK)
            score = (scores[0][..., :, None] + scores[1][..., None, :]).reshape(b, n, HEADS, PK_TOPK * PK_TOPK)
            final_scores, pk_idx = jax.lax.top_k(score, FINAL_TOPK)
            final_indices = jnp.take_along_axis(index, pk_idx, axis=-1)
            final_scores = jax.nn.softmax(final_scores, axis=-1)
            return (final_scores, final_indices)
        key = jax.random.key(seed)
        ks = jax.random.split(key, 7)
        b, n = (2, 256)
        std = 0.02
        x = jax.random.normal(ks[0], (b, n, DIM), dtype=jnp.float32)
        Wq_pk = jax.random.normal(ks[1], (DIM, P * HEADS * DIM_KEY), dtype=jnp.float32) * std
        pk_keys = jax.random.normal(ks[2], (P, NUM_KEYS, HEADS, DIM_KEY), dtype=jnp.float32) * std
        Wq = jax.random.normal(ks[3], (DIM, HEADS * DIM), dtype=jnp.float32) * std
        keys_table = jax.random.normal(ks[4], (NUM_KV * HEADS, DIM), dtype=jnp.float32) * std
        values_table = jax.random.normal(ks[5], (NUM_KV * HEADS, DIM), dtype=jnp.float32) * std
        Wo = jax.random.normal(ks[6], (DIM * HEADS, DIM), dtype=jnp.float32) * std
        return {'x': x, 'Wq_pk': Wq_pk, 'pk_keys': pk_keys, 'Wq': Wq, 'keys_table': keys_table, 'values_table': values_table, 'Wo': Wo}
    _L0_ffn_all = _L0_ffn_setup()
    _L0_ffn_in = {k: v for k, v in _L0_ffn_all.items() if k in ('Wq_pk', 'pk_keys', 'Wq', 'keys_table', 'values_table', 'Wo')}
    del _L0_ffn_all
    return {'x': x, 'cls_tok': cls_tok, 'L0_tok_W': _L0_tok_in['W'], 'L0_tok_b': _L0_tok_in['b'], 'L0_attn_qkv_w': _L0_attn_in['qkv_w'], 'L0_attn_qkv_b': _L0_attn_in['qkv_b'], 'L0_attn_proj_w': _L0_attn_in['proj_w'], 'L0_attn_proj_b': _L0_attn_in['proj_b'], 'L0_attn_logit_scale': _L0_attn_in['logit_scale'], 'L0_attn_mlp1_w': _L0_attn_in['mlp1_w'], 'L0_attn_mlp1_b': _L0_attn_in['mlp1_b'], 'L0_attn_mlp2_w': _L0_attn_in['mlp2_w'], 'L0_attn_mlp2_b': _L0_attn_in['mlp2_b'], 'L0_ffn_Wq_pk': _L0_ffn_in['Wq_pk'], 'L0_ffn_pk_keys': _L0_ffn_in['pk_keys'], 'L0_ffn_Wq': _L0_ffn_in['Wq'], 'L0_ffn_keys_table': _L0_ffn_in['keys_table'], 'L0_ffn_values_table': _L0_ffn_in['values_table'], 'L0_ffn_Wo': _L0_ffn_in['Wo']}

def reference(x, cls_tok, L0_tok_W, L0_tok_b, L0_attn_qkv_w, L0_attn_qkv_b, L0_attn_proj_w, L0_attn_proj_b, L0_attn_logit_scale, L0_attn_mlp1_w, L0_attn_mlp1_b, L0_attn_mlp2_w, L0_attn_mlp2_b, L0_ffn_Wq_pk, L0_ffn_pk_keys, L0_ffn_Wq, L0_ffn_keys_table, L0_ffn_values_table, L0_ffn_Wo):
    import jax
    import jax.numpy as jnp

    def _L0_tok_ref(x, W, b):
        import jax, jax.numpy as jnp
        import numpy as np
        INV_SQRT2 = 0.7071067811865476

        def haar_dwt2(x):
            lo = (x[..., ::2] + x[..., 1::2]) * INV_SQRT2
            hi = (x[..., ::2] - x[..., 1::2]) * INV_SQRT2
            cA = (lo[..., ::2, :] + lo[..., 1::2, :]) * INV_SQRT2
            cH = (lo[..., ::2, :] - lo[..., 1::2, :]) * INV_SQRT2
            cV = (hi[..., ::2, :] + hi[..., 1::2, :]) * INV_SQRT2
            cD = (hi[..., ::2, :] - hi[..., 1::2, :]) * INV_SQRT2
            return (cA, (cH, cV, cD))

        def wavedec2_maps(x, levels):
            a = x
            details = []
            for _ in range(levels):
                a, d = haar_dwt2(a)
                details.append(d)
            maps = [a]
            for d in reversed(details):
                maps.extend(d)
            return maps
        imgs = x[:, 0]
        B = imgs.shape[0]
        maps = wavedec2_maps(imgs, 2)
        proc = [jax.image.resize(m, (B, 8, 8), method='bilinear') for m in maps]
        feat = jnp.stack(proc, axis=1)
        feat = feat.reshape(B, feat.shape[1], 64).transpose(0, 2, 1)
        return feat @ W + b

    def _L0_attn_ref(x, qkv_w, qkv_b, proj_w, proj_b, logit_scale, mlp1_w, mlp1_b, mlp2_w, mlp2_b):
        import jax, jax.numpy as jnp
        import numpy as np
        import math
        B, L, C = (1024, 64, 64)
        H = 8
        META_H = 96

        def _rel_coords_log(W):
            c0 = jnp.zeros((W,), jnp.float32)
            c1 = jnp.arange(W, dtype=jnp.float32)
            coords = jnp.stack([c0, c1], axis=0)
            rel = coords[:, :, None] - coords[:, None, :]
            rel = rel.transpose(1, 2, 0).reshape(-1, 2)
            return jnp.sign(rel) * jnp.log1p(jnp.abs(rel))
        b, l, c = x.shape
        h = H
        d = c // h
        qkv = x @ qkv_w.T + qkv_b
        qkv = qkv.reshape(b, l, 3, h, d).transpose(2, 0, 3, 1, 4)
        q, k, v = (qkv[0], qkv[1], qkv[2])
        qn = q / jnp.maximum(jnp.linalg.norm(q, axis=-1, keepdims=True), 1e-12)
        kn = k / jnp.maximum(jnp.linalg.norm(k, axis=-1, keepdims=True), 1e-12)
        attn = jnp.einsum('bhld,bhmd->bhlm', qn, kn)
        scale = jnp.exp(jnp.minimum(logit_scale, math.log(1.0 / 0.01)))
        attn = attn * scale.reshape(1, h, 1, 1)
        rel = _rel_coords_log(l)
        hid = jax.nn.relu(rel @ mlp1_w.T + mlp1_b)
        bias = (hid @ mlp2_w.T + mlp2_b).T.reshape(h, l, l)
        attn = jax.nn.softmax(attn + bias[None], axis=-1)
        out = jnp.einsum('bhlm,bhmd->bhld', attn, v)
        out = out.transpose(0, 2, 1, 3).reshape(b, l, c)
        return out @ proj_w.T + proj_b

    def _L0_ffn_ref(x, Wq_pk, pk_keys, Wq, keys_table, values_table, Wo):
        import jax, jax.numpy as jnp
        import numpy as np
        DIM = 64
        HEADS = 8
        NUM_KEYS = 64
        NUM_KV = NUM_KEYS ** 2
        PK_TOPK = 16
        FINAL_TOPK = 16
        DIM_KEY = DIM // 2
        P = 2

        def _pk(x, Wq_pk, pk_keys):
            b, n, _ = x.shape
            q = (x @ Wq_pk).reshape(b, n, P, HEADS, DIM_KEY).transpose(2, 0, 1, 3, 4)
            sim = jnp.einsum('pbnhd,pkhd->pbnhk', q, pk_keys)
            scores, idx = jax.lax.top_k(sim, PK_TOPK)
            idx0 = idx[0]
            idx1 = idx[1] * NUM_KEYS
            index = (idx0[..., :, None] + idx1[..., None, :]).reshape(b, n, HEADS, PK_TOPK * PK_TOPK)
            score = (scores[0][..., :, None] + scores[1][..., None, :]).reshape(b, n, HEADS, PK_TOPK * PK_TOPK)
            final_scores, pk_idx = jax.lax.top_k(score, FINAL_TOPK)
            final_indices = jnp.take_along_axis(index, pk_idx, axis=-1)
            final_scores = jax.nn.softmax(final_scores, axis=-1)
            return (final_scores, final_indices)
        b, n, d = x.shape
        q = (x @ Wq).reshape(b, n, HEADS, DIM) * DIM ** (-0.5)
        kv_scores, indices = _pk(x, Wq_pk, pk_keys)
        offsets = jnp.arange(HEADS, dtype=indices.dtype) * NUM_KV
        ind = indices + offsets[None, None, :, None]
        k = jnp.einsum('bnhk,bnhkd->bnhd', kv_scores, keys_table[ind])
        v = jnp.einsum('bnhk,bnhkd->bnhd', kv_scores, values_table[ind])
        sim = jnp.einsum('bihd,bjhd->bhij', q, k)
        neg = -jnp.finfo(sim.dtype).max
        causal = jnp.tril(jnp.ones((n, n), dtype=bool))
        sim = jnp.where(causal, sim, neg)
        attn = jax.nn.softmax(sim, axis=-1)
        out = jnp.einsum('bhij,bjhd->bhid', attn, v)
        out = out.transpose(0, 2, 1, 3).reshape(b, n, HEADS * DIM)
        return out @ Wo
    h = _L0_tok_ref(x, L0_tok_W, L0_tok_b)
    h = jnp.concatenate([jnp.broadcast_to(cls_tok, (h.shape[0], 1, h.shape[2])), h], axis=1)
    h = h + _L0_attn_ref(_layernorm(h, axis=-1), L0_attn_qkv_w, L0_attn_qkv_b, L0_attn_proj_w, L0_attn_proj_b, L0_attn_logit_scale, L0_attn_mlp1_w, L0_attn_mlp1_b, L0_attn_mlp2_w, L0_attn_mlp2_b)
    h = h + _L0_ffn_ref(_layernorm(h, axis=-1), L0_ffn_Wq_pk, L0_ffn_pk_keys, L0_ffn_Wq, L0_ffn_keys_table, L0_ffn_values_table, L0_ffn_Wo)
    return h

_drawn_inputs = setup_inputs


def setup_inputs(seed=0):
    import zlib

    import numpy as np

    out = dict(_drawn_inputs(seed))
    spreads = {'L0_tok_b': (0.0, 0.1),
     'L0_attn_qkv_b': (0.0, 0.1),
     'L0_attn_proj_b': (0.0, 0.1),
     'L0_attn_logit_scale': (2.3025851249694824, 0.6),
     'L0_attn_mlp1_b': (0.0, 2.0),
     'L0_attn_mlp2_b': (0.0, 2.0)}
    factors = {'cls_tok': 2.823,
     'L0_attn_mlp1_w': 27.945,
     'L0_attn_mlp2_w': 30.283,
     'L0_ffn_Wq_pk': 8.0,
     'L0_ffn_pk_keys': 8.0,
     'L0_ffn_Wq': 47.132,
     'L0_ffn_keys_table': 50.491,
     'L0_ffn_values_table': 8.0,
     'L0_ffn_Wo': 8.0}
    for name, (base, spread) in spreads.items():
        noise = np.random.default_rng([zlib.crc32(name.encode()), seed]).standard_normal(out[name].shape)
        drawn = base * np.exp(spread * noise) if base else spread * noise
        out[name] = jnp.asarray(drawn.astype(out[name].dtype))
    for name, factor in factors.items():
        out[name] = (out[name] * factor).astype(out[name].dtype)
    return out
```

```python
from contextlib import ExitStack

import numpy as np

import concourse.bass as bass
from concourse import mybir

F32 = mybir.dt.float32
F32R = mybir.dt.float32r
ALU = mybir.AluOpType
ACT = mybir.ActivationFunctionType
AX = mybir.AxisListType

B, IMG, C = 64, 112, 64
GRID = 8
L = GRID * GRID + 1
H, HD = 8, 8
META = 96
NK, DK, TOPK = 64, 32, 16
NB = 8
T = NB * L
ITERS = B // NB
HALF = T // 2
TT, NT = T // 5, 5
CH = NK * NK // 128
UNITS = CH
R0 = 4
R1 = 3
NCAND = R0 * TOPK + (TOPK - R0) * R1
LOWEST = -3.0e38
MASKED = -1.0e30
EXP_CAP = 80.0
ROUNDING = 2.0 ** -20
EPS = 1e-5
SCALE2 = float(C) ** -0.5


def shape_constants():
    def resize(n):
        scale = n / GRID
        x = (np.arange(GRID) + 0.5) * scale - 0.5
        w = np.maximum(0.0, 1.0 - np.abs(x[:, None] - np.arange(n)[None, :]) / scale)
        return w / w.sum(axis=1, keepdims=True)

    def haar(n):
        lo, hi = np.zeros((n // 2, n)), np.zeros((n // 2, n))
        i = np.arange(n // 2)
        lo[i, 2 * i] = lo[i, 2 * i + 1] = hi[i, 2 * i] = 0.7071067811865476
        hi[i, 2 * i + 1] = -0.7071067811865476
        return lo, hi

    lo1, hi1 = haar(IMG)
    lo2, hi2 = haar(IMG // 2)
    r1, r2 = resize(IMG // 2), resize(IMG // 4)
    filters = np.concatenate([r2 @ lo2 @ lo1, r2 @ hi2 @ lo1, r1 @ lo1, r1 @ hi1])
    d = np.arange(-(L - 1), L)
    rel = np.stack([0.0 * d, np.sign(d) * np.log1p(np.abs(d)), np.ones(len(d))])
    part = np.arange(128)
    spread = np.zeros((128, CH, 128))
    for c in range(CH):
        spread[part % NK, c, part] = 1.0
        spread[NK + 2 * c + part // NK, c, part] = 1.0
    causal = np.where(np.arange(L)[None, :] <= np.arange(L)[:, None], 0.0, MASKED)
    return {
        "filters": filters.T,
        "rel": rel,
        "spread": spread.reshape(128, CH * 128),
        "ident": np.eye(128),
        "head_sum": np.kron(np.eye(16), np.ones((8, 8))),
        "center": np.eye(C) - 1.0 / C,
        "mean": np.full((C, C), 1.0 / C),
        "head_mask": np.kron(np.eye(H), np.ones((HD, 1))),
        "causal": causal,
    }


def build(nc, d):
    with ExitStack() as ctx:
        def sb(name, shape, dt=F32):
            return ctx.enter_context(nc.sbuf_tensor(name, shape, dt))

        body_sems = []

        def bsem(name):
            s = ctx.enter_context(nc.semaphore(name))
            body_sems.append(s)
            return s

        image_in = bsem("image_in")
        rows_mm, rows_out = bsem("rows_mm"), bsem("rows_out")
        maps_mm, maps_out = bsem("maps_mm"), bsem("maps_out")
        tok_mm, cls_set, h1_ready = bsem("tok_mm"), bsem("cls_set"), bsem("h1_ready")
        cen_mm, sq_ready, var_mm, std_ready, ln_ready = (
            bsem("cen_mm"), bsem("sq_ready"), bsem("var_mm"), bsem("std_ready"), bsem("ln_ready"))
        qk_mm, qk_out, qk_sq, nrm_mm, nrm_ready, qk_unit = (
            bsem("qk_mm"), bsem("qk_out"), bsem("qk_sq"), bsem("nrm_mm"), bsem("nrm_ready"), bsem("qk_unit"))
        v_mm, v_out, kx_ready = bsem("v_mm"), bsem("v_out"), bsem("kx_ready")
        s_mm, s_sub, s_exp, pt_mm, pt_out = (
            bsem("s_mm"), bsem("s_sub"), bsem("s_exp"), bsem("pt_mm"), bsem("pt_out"))
        o_mm, o_out, ot_mm, ot_out, proj_mm, h2_ready = (
            bsem("o_mm"), bsem("o_out"), bsem("ot_mm"), bsem("ot_out"), bsem("proj_mm"), bsem("h2_ready"))
        dve_link = bsem("dve_link")
        sc_mm, sc_out, shift_ready, z_ready, rz_ready, st_mm, hi_ready, st_ready = (
            bsem("sc_mm"), bsem("sc_out"), bsem("shift_ready"), bsem("z_ready"), bsem("rz_ready"),
            bsem("st_mm"), bsem("hi_ready"), bsem("st_ready"))
        a_ready, e_ready, w_ready, out_done, kv_ready = (
            bsem("a_ready"), bsem("e_ready"), bsem("w_ready"), bsem("out_done"), bsem("kv_ready"))
        q2_mm, q2_out, s2_mm, s2_sub, s2_exp, p2_ready, pt2_mm, pt2_out = (
            bsem("q2_mm"), bsem("q2_out"), bsem("s2_mm"), bsem("s2_sub"), bsem("s2_exp"),
            bsem("p2_ready"), bsem("pt2_mm"), bsem("pt2_out"))
        v2_mm, v2_out, o2_mm, o2_out, ffn_mm, ffn_added = (
            bsem("v2_mm"), bsem("v2_out"), bsem("o2_mm"), bsem("o2_out"), bsem("ffn_mm"), bsem("ffn_added"))
        y_mm, y_out, y_stored = bsem("y_mm"), bsem("y_out"), bsem("y_stored")

        def sem(name):
            return ctx.enter_context(nc.semaphore(name))

        consts_in, spread_in = sem("consts_in"), sem("spread_in")
        tables_in = [sem(f"table{h}_in") for h in range(H)]
        set_mm, set_act, set_dve = sem("set_mm"), sem("set_act"), sem("set_dve")
        eps_set = sem("eps_set")
        iter_end, iter_clear = sem("iter_end"), sem("iter_clear")

        table = sb("table", [128, H, CH, 128])
        spread = sb("spread", [128, CH * 128], F32R)
        spread_f = table[:, H - 1, :, :].rearrange("p c n -> p (c n)")
        ident = sb("ident", [128, 128])
        filters = sb("filters", [IMG, 32])
        w_tok = sb("w_tok", [32, GRID, 4, C])
        tok_b, cls_tok = sb("tok_b", [C, 1]), sb("cls_tok", [C, 1])
        center, mean = sb("center", [C, C]), sb("mean", [C, C])
        head_sum = sb("head_sum", [128, 128])
        head_mask = sb("head_mask", [C, H])
        w_qk, b_qk = sb("w_qk", [C, 128]), sb("b_qk", [128, 1])
        w_v, b_v = sb("w_v", [C, C]), sb("b_v", [L, C])
        w_proj, b_proj = sb("w_proj", [C, C]), sb("b_proj", [C, 1])
        q_scale = sb("q_scale", [C, 1])
        rel, mlp1, mlp2 = sb("rel", [3, 2 * L - 1]), sb("mlp1", [3, META]), sb("mlp2", [META + 1, H])
        hid = sb("hid", [META + 1, 2 * L - 1])
        pos_bias = sb("pos_bias", [L, H, L])
        causal = sb("causal", [L, L])
        pk_q, pk_k = (table[0:DK, H - 2, 0:8, :].rearrange("p c n -> p (c n)").rearrange("p (g n) -> p g n", g=16),
                      table[0:DK, H - 2, 8:16, :].rearrange("p c n -> p (c n)").rearrange("p (g n) -> p g n", g=16))
        w_sim = sb("w_sim", [C, H, 2 * NK])
        w_q2, w_o2 = sb("w_q2", [C, H * C]), sb("w_o2", [C, H, C])
        eps = sb("eps", [128, 1])

        h_sb, xh = sb("h_sb", [C, T]), sb("xh", [C, T])
        expo = sb("expo", [128, 2, T])
        wts = sb("wts", [128, 2, T])
        kv = sb("kv", [128, 2, T])
        rz_row = sb("rz_row", [128, 2, T])
        st_hi, st_lo = sb("st_hi", [128, 2, T], F32R), sb("st_lo", [128, 2, T], F32R)
        q2, s2, pt2, o2 = sb("q2", [128, T]), sb("s2", [128, T]), sb("pt2", [128, T]), sb("o2", [128, T])
        v2 = sb("v2", [L, NB, C])
        sc = sb("sc", [TT, 2, 2 * NK])
        best = sb("best", [TT, 2, TOPK])
        rest = sb("rest", [TT, NCAND])
        cand = sb("cand", [TT, NCAND])
        top = sb("top", [TT, 2, 24])
        stat = sb("stat", [TT, 2, 4])
        cand_e = sb("cand_e", [TT, TOPK])
        red = sb("red", [L, 2, 16])
        image = kv[0:IMG, :, :].rearrange("p a t -> p (a t)")[:, 0:NB * IMG].rearrange("p (b x) -> p b x", b=NB)
        rows = expo[0:IMG, 0, 0:NB * 32]
        maps = expo[0:32, 1, 0:NB * 32]
        qn, kn = rz_row[0:C, 0, :], rz_row[0:C, 1, :]
        kx = wts[0:C, :, :].rearrange("p a (h m) -> p a h m", h=H)
        y_sb = s2[0:TT, 0:NT * C]
        ps = ctx.enter_context(nc.psum_tensor("ps", [128, 8, 512], F32))

        def pair(k, parts, n=HALF):
            return ps[0:parts, k:k + 2, 0:n]

        def halves(ap):
            return ap.rearrange("p (s t) -> p s t", s=2)

        def both(eng_mm, bank, parts, lhsT, rhs, sem_):
            for s in range(2):
                mm = eng_mm(ps[0:parts, bank + s, 0:HALF], lhsT, rhs[:, s * HALF:(s + 1) * HALF],
                            start=True, stop=True)
            mm.then_inc(sem_, 1)

        x_v = d["x"].rearrange("b c y x -> y (b c) x")
        out_v = d["out"].rearrange("(i j) n c -> i (j n) c", j=NB).rearrange("i (t p) c -> i p t c", p=TT)

        consts = [(ident, "ident"), (filters, "filters"), (tok_b, "tok_b"), (cls_tok, "cls_tok"),
                  (center, "center"), (mean, "mean"), (head_sum, "head_sum"), (head_mask, "head_mask"),
                  (w_qk, "w_qk"), (b_qk, "b_qk"), (w_v, "w_v"), (b_v, "b_v"), (w_proj, "w_proj"),
                  (b_proj, "b_proj"), (q_scale, "q_scale"), (rel, "rel"), (mlp1, "mlp1"), (mlp2, "mlp2"),
                  (causal, "causal"), (w_q2, "w_q2")]
        N_CONSTS = len(consts) + 4

        block = ctx.enter_context(nc.Block())

        @block.sync
        def _(sp):
            for tile, name in consts:
                sp.dma_start(tile[:, :], d[name]).then_inc(consts_in, 16)
            sp.dma_start(w_tok[:, :, :, :].rearrange("p j r c -> p (j r c)"), d["w_tok"]).then_inc(consts_in, 16)
            sp.dma_start(w_o2[:, :, :].rearrange("p h c -> p (h c)"), d["w_o2"]).then_inc(consts_in, 16)
            sp.dma_start(pk_q, d["pk_q"]).then_inc(consts_in, 16)
            sp.dma_start(pk_k, d["pk_k"]).then_inc(consts_in, 16)
            sp.dma_start(spread_f, d["spread"]).then_inc(spread_in, 16)
            for h in range(H - 2):
                sp.dma_start(table[:, h, :, :].rearrange("p c n -> p (c n)"), d["table"][:, h, :])\
                  .then_inc(tables_in[h], 16)
            sp.wait_ge(consts_in, 16 * N_CONSTS)
            sp.wait_ge(spread_in, 16)
            sp.wait_ge(set_mm, 2)
            sp.wait_ge(set_dve, 2)
            for h in range(H - 2, H):
                sp.dma_start(table[:, h, :, :].rearrange("p c n -> p (c n)"), d["table"][:, h, :])\
                  .then_inc(tables_in[h], 16)
            with sp.Fori(0, ITERS) as it:
                sp.dma_start(image, x_v[:, bass.ds(it * NB, NB), :]).then_inc(image_in, 16)
                sp.wait_ge(y_out, 1)
                sp.dma_start(out_v[bass.ds(it, 1), :, :, :].rearrange("i p t c -> (i p) t c"),
                             y_sb.rearrange("p (t c) -> p t c", t=NT)).then_inc(y_stored, 16)
                sp.wait_ge(y_stored, 16)
                sp.drain().then_inc(iter_end, 1)
                sp.wait_ge(iter_clear, it + 1)
                sp.nop(nofuse=True)

        @block.gpsimd
        def _(pool):
            nc.gpsimd.memset(eps[:, :], EPS).then_inc(eps_set, 1)
            pool.wait_ge(consts_in, 16 * N_CONSTS)
            with pool.Fori(0, ITERS) as it:
                for b in range(NB):
                    pool.wait_ge(qk_unit, 2)
                    if b >= 2:
                        pool.wait_ge(s_mm, b - 1)
                    nc.gpsimd.tensor_tensor(
                        kx[:, b % 2, :, :],
                        kn[:, b * L:(b + 1) * L].unsqueeze(1).to_broadcast([C, H, L]),
                        head_mask[:, :].unsqueeze(2).to_broadcast([C, H, L]), ALU.mult).then_inc(kx_ready, 1)
                pool.wait_ge(iter_end, it * 4 + 4)
                pool.nop(nofuse=True)
                for s in body_sems:
                    pool.sem_clear(s)
                pool.nop().then_inc(iter_clear, 1)

        @block.tensor
        def _(pe):
            mm = nc.tensor.matmul
            tr = nc.tensor.transpose
            pe.wait_ge(consts_in, 16 * N_CONSTS)
            mm(ps[0:META, 0, 0:2 * L - 1], mlp1[:, :], rel[:, :], start=True, stop=True).then_inc(set_mm, 1)
            for g in range(2 * H):
                last = mm(ps[0:C, 2 + g // 8, (g % 8) * NK:(g % 8 + 1) * NK], pk_q[:, g, :], pk_k[:, g, :],
                          start=True, stop=True)
            last.then_inc(set_mm, 1)
            pe.wait_ge(set_act, 1)
            pe.wait_ge(set_dve, 1)
            for m in range(L):
                last = mm(ps[0:L, 4 + m // NK, (m % NK) * H:(m % NK + 1) * H], hid[:, L - 1 - m:2 * L - 1 - m],
                          mlp2[:, :], start=True, stop=True)
            last.then_inc(set_mm, 1)
            pe.wait_ge(set_act, 4)

            with pe.Fori(0, ITERS) as it:
                pe.wait_ge(image_in, 16)
                for b in range(NB):
                    last = mm(ps[0:IMG, 6, b * 32:(b + 1) * 32], image[:, b, :], filters[:, :], start=True, stop=True)
                last.then_inc(rows_mm, 1)
                pe.wait_ge(rows_out, 1)
                mm(ps[0:32, 7, 0:NB * 32], filters[:, :], rows, start=True, stop=True).then_inc(maps_mm, 1)
                pe.wait_ge(maps_out, 1)
                maps_v = maps.rearrange("p (b r i) -> p b r i", b=NB, r=4)
                for j in range(GRID):
                    for r in range(4):
                        last = mm(ps[0:C, 6, j * 64:(j + 1) * 64], w_tok[:, j, r, :], maps_v[:, :, r, :],
                                  start=(r == 0), stop=(r == 3))
                last.then_inc(tok_mm, 1)

                def layernorm(n):
                    if n == 0:
                        pe.wait_ge(h1_ready, 1)
                        pe.wait_ge(cls_set, 1)
                    else:
                        pe.wait_ge(h2_ready, 1)
                    both(mm, 0, C, center[:, :], h_sb[:, :], cen_mm)
                    pe.wait_ge(sq_ready, n + 1)
                    both(mm, 2, C, mean[:, :], s2[0:C, :], var_mm)

                layernorm(0)
                pe.wait_ge(ln_ready, 1)
                both(mm, 4, 128, w_qk[:, :], xh[:, :], qk_mm)
                for b in range(NB):
                    last = mm(ps[0:L, 0, b * C:(b + 1) * C], xh[:, b * L:(b + 1) * L], w_v[:, :],
                              start=True, stop=True)
                last.then_inc(v_mm, 1)
                pe.wait_ge(qk_sq, 1)
                both(mm, 6, 128, head_sum[:, :], s2[:, :], nrm_mm)

                def a1_scores(b):
                    pe.wait_ge(kx_ready, b + 1)
                    if b == 0:
                        pe.wait_ge(v_out, 1)
                    if b >= 2:
                        pe.wait_ge(s_sub, 2 * b - 3)
                    bank = 2 * (b % 2)
                    for s in range(2):
                        last = mm(ps[0:L, bank + s, 0:HALF], qn[:, b * L:(b + 1) * L],
                                  kx[:, b % 2, 4 * s:4 * s + 4, :].rearrange("p h m -> p (h m)"), start=True, stop=True)
                    last.then_inc(s_mm, 1)

                def a1_turn(b):
                    pe.wait_ge(s_exp, b + 1)
                    if b >= 1:
                        pe.wait_ge(pt_out, b)
                    e = expo[0:L, b % 2, :].rearrange("p (h m) -> p h m", h=H)
                    for h in range(H):
                        last = tr(ps[0:L, 4 + h // 4, (h % 4) * L:(h % 4 + 1) * L], e[:, h, :], ident[0:L, 0:L])
                    last.then_inc(pt_mm, 1)

                def a1_values(b):
                    pe.wait_ge(pt_out, b + 1)
                    if b >= 1:
                        pe.wait_ge(o_out, b)
                    pt = kv[0:L, b % 2, :].rearrange("p (h l) -> p h l", h=H)
                    for h in range(H):
                        last = mm(ps[0:L, 6, h * HD:(h + 1) * HD], pt[:, h, :], v2[:, b, h * HD:(h + 1) * HD],
                                  start=True, stop=True)
                    last.then_inc(o_mm, 1)

                def a1_back(b):
                    pe.wait_ge(o_out, b + 1)
                    if b >= 1:
                        pe.wait_ge(ot_out, b)
                    tr(ps[0:C, 7, 0:L], s2[0:L, (b % 2) * C:(b % 2 + 1) * C], ident[0:L, 0:L]).then_inc(ot_mm, 1)

                pe.wait_ge(nrm_ready, 1)
                for slot in range(NB + 4):
                    if slot < NB:
                        a1_scores(slot)
                    if 1 <= slot <= NB:
                        a1_turn(slot - 1)
                    if 2 <= slot <= NB + 1:
                        a1_values(slot - 2)
                    if 3 <= slot <= NB + 2:
                        a1_back(slot - 3)
                pe.wait_ge(ot_out, NB)
                both(mm, 0, C, w_proj[:, :], o2[0:C, :], proj_mm)
                layernorm(1)
                pe.wait_ge(ln_ready, 2)

                def scores(h, t):
                    n = NT * h + t
                    if n >= 1:
                        pe.wait_ge(sc_out, n)
                    if n >= 2:
                        pe.wait_ge(st_ready, n - 1)
                    mm(ps[0:TT, 5, 0:128], xh[:, t * TT:(t + 1) * TT], w_sim[:, h, :],
                       start=True, stop=True).then_inc(sc_mm, 1)

                def turn_scores(h, t):
                    n = NT * h + t
                    pe.wait_ge(rz_ready, n + 1)
                    if t < NT - 1:
                        pe.wait_ge(sc_out, n + 2)
                    tr(ps[0:128, 5, 128:128 + TT], sc[:, n % 2, :], ident[0:TT, 0:TT])
                    mm(ps[0:128, 5, 256:256 + TT], stat[:, n % 2, 3:4].to_broadcast([TT, 128]), ident[0:TT, 0:TT],
                       start=True, stop=True).then_inc(st_mm, 1)

                def spread_scores(g):
                    h, u = g // UNITS, g % UNITS
                    s, cp = u // (CH // 2), u % (CH // 2)
                    if u == 0:
                        pe.wait_ge(st_ready, NT * (h + 1))
                    if g >= 2:
                        pe.wait_ge(w_ready, g - 1)
                    for k in range(2):
                        w = spread[:, (2 * cp + k) * 128:(2 * cp + k + 1) * 128]
                        o = ps[0:128, 2 * (g % 2) + k, 0:HALF]
                        mm(o, w, st_hi[:, h % 2, s * HALF:(s + 1) * HALF], start=True, stop=False)
                        last = mm(o, w, st_lo[:, h % 2, s * HALF:(s + 1) * HALF], start=False, stop=True)
                    last.then_inc(a_ready, 1)

                def add_rows(g):
                    h, u = g // UNITS, g % UNITS
                    cp = u % (CH // 2)
                    pe.wait_ge(w_ready, g + 1)
                    pe.wait_ge(tables_in[h], 16)
                    if cp == 0 and g > 0:
                        pe.wait_ge(kv_ready, g // (CH // 2))
                    for k in range(2):
                        last = mm(ps[0:128, 4, 0:HALF], table[:, h, 2 * cp + k, :],
                                  wts[:, g % 2, k * HALF:(k + 1) * HALF],
                                  start=(cp == 0 and k == 0), stop=(cp == CH // 2 - 1 and k == 1))
                    last.then_inc(out_done, 1)

                def attend(h, u):
                    if u == 0:
                        if h > 0:
                            pe.wait_ge(ffn_added, h)
                        both(mm, 6, C, w_q2[:, h * C:(h + 1) * C], xh[:, :], q2_mm)
                    if u == 2:
                        pe.wait_ge(q2_out, h + 1)
                        pe.wait_ge(kv_ready, 2 * h + 2)
                        for b in range(NB):
                            last = mm(ps[0:L, 6 + b // 4, (b % 4) * L:(b % 4 + 1) * L], q2[0:C, b * L:(b + 1) * L],
                                      kv[0:C, h % 2, b * L:(b + 1) * L], start=True, stop=True)
                        last.then_inc(s2_mm, 1)
                    if u == 10:
                        pe.wait_ge(p2_ready, h + 1)
                        for b in range(NB):
                            last = tr(ps[0:L, 6 + b // 4, (b % 4) * L:(b % 4 + 1) * L],
                                      s2[0:L, b * L:(b + 1) * L], ident[0:L, 0:L])
                        last.then_inc(pt2_mm, 1)
                    if u == 12:
                        pe.wait_ge(pt2_out, h + 1)
                        for b in range(NB):
                            last = tr(ps[0:L, 6, b * C:(b + 1) * C], kv[C:128, h % 2, b * L:(b + 1) * L],
                                      ident[C:128, C:128])
                        last.then_inc(v2_mm, 1)
                    if u == 14:
                        pe.wait_ge(v2_out, h + 1)
                        for b in range(NB):
                            last = mm(ps[0:C, 6 + b // 4, (b % 4) * L:(b % 4 + 1) * L], v2[:, b, :],
                                      pt2[0:L, b * L:(b + 1) * L], start=True, stop=True)
                        last.then_inc(o2_mm, 1)
                    if u == 16:
                        pe.wait_ge(o2_out, h + 1)
                        both(mm, 6, C, w_o2[:, h, :], o2[0:C, :], ffn_mm)

                for hh in range(-1, H + 1):
                    for u in range(UNITS):
                        g = hh * UNITS + u
                        if 0 <= g + 1 < H * UNITS:
                            spread_scores(g + 1)
                        if 0 <= g - 1 < H * UNITS:
                            add_rows(g - 1)
                        if hh + 1 < H and u % 5 == 0 and u // 5 < NT:
                            scores(hh + 1, u // 5)
                        if hh + 1 < H and u >= 6 and (u - 6) % 5 == 0 and (u - 6) // 5 < NT:
                            turn_scores(hh + 1, (u - 6) // 5)
                        if hh >= 1:
                            attend(hh - 1, u)
                pe.wait_ge(ffn_added, H)
                for t in range(NT):
                    last = tr(ps[0:TT, 6, t * C:(t + 1) * C], h_sb[:, t * TT:(t + 1) * TT], ident[0:C, 0:C])
                last.then_inc(y_mm, 1)
                pe.drain().then_inc(iter_end, 1)
                pe.wait_ge(iter_clear, it + 1)

        @block.scalar
        def _(act):
            A = nc.scalar.activation
            act.wait_ge(set_mm, 1)
            A(hid[0:META, :], ps[0:META, 0, 0:2 * L - 1], ACT.Relu).then_inc(set_act, 1)
            act.wait_ge(set_mm, 2)
            A(w_sim[:, :, :].rearrange("p h n -> p (h n)"),
              ps[0:C, 2:4, :].rearrange("p a n -> p (a n)"), ACT.Copy).then_inc(set_act, 1)
            act.wait_ge(set_mm, 3)
            A(pos_bias[:, :, 0:NK], ps[0:L, 4, :].rearrange("p (m h) -> p h m", h=H), ACT.Copy)\
                .then_inc(set_act, 1)
            A(pos_bias[:, :, NK:L], ps[0:L, 5, 0:H].rearrange("p (m h) -> p h m", h=H), ACT.Copy)\
                .then_inc(set_act, 1)
            act.wait_ge(set_dve, 3)
            A(q_scale[:, :], q_scale[:, :], ACT.Exp).then_inc(set_act, 1)

            with act.Fori(0, ITERS) as it:
                act.wait_ge(rows_mm, 1)
                A(rows, ps[0:IMG, 6, 0:NB * 32], ACT.Copy).then_inc(rows_out, 1)
                act.wait_ge(maps_mm, 1)
                A(maps, ps[0:32, 7, 0:NB * 32], ACT.Copy).then_inc(maps_out, 1)
                act.wait_ge(tok_mm, 1)
                h_tok = h_sb[:, :].rearrange("p (b n) -> p b n", b=NB)[:, :, 1:L]\
                    .rearrange("p b (i j) -> p j b i", j=GRID)
                tok = ps[0:C, 6, :].rearrange("p (j b i) -> p j b i", j=GRID, b=NB)
                for j in range(GRID):
                    last = A(h_tok[:, j, :, :], tok[:, j, :, :], ACT.Identity, bias=tok_b[:, 0:1])
                last.then_inc(h1_ready, 1)

                def layernorm(n):
                    act.wait_ge(cen_mm, n + 1)
                    A(halves(s2[0:C, :]), pair(0, C), ACT.Square).then_inc(sq_ready, 1)
                    act.wait_ge(eps_set, 1)
                    act.wait_ge(var_mm, n + 1)
                    A(halves(pt2[0:C, :]), pair(2, C), ACT.Sqrt, bias=eps[0:C, 0:1]).then_inc(std_ready, 1)

                layernorm(0)
                act.wait_ge(qk_mm, 1)
                A(halves(q2[:, :]), pair(4, 128), ACT.Identity, bias=b_qk[:, 0:1]).then_inc(qk_out, 1)
                act.wait_ge(qk_out, 1)
                A(s2[:, :], q2[:, :], ACT.Square).then_inc(qk_sq, 1)
                act.wait_ge(nrm_mm, 1)
                act.wait_ge(ln_ready, 1)
                A(halves(pt2[:, :]), pair(6, 128), ACT.Sqrt).then_inc(nrm_ready, 1)

                def a1_exp(b):
                    act.wait_ge(s_sub, 2 * b + 2)
                    A(expo[0:L, b % 2, :], expo[0:L, b % 2, :], ACT.Exp).then_inc(s_exp, 1)

                def a1_turned(b):
                    act.wait_ge(pt_mm, b + 1)
                    if b >= 2:
                        act.wait_ge(o_mm, b - 1)
                    A(halves(kv[0:L, b % 2, :]), pair(4, L), ACT.Copy).then_inc(pt_out, 1)

                def a1_back(b):
                    act.wait_ge(ot_mm, b + 1)
                    A(o2[0:C, b * L:(b + 1) * L], ps[0:C, 7, 0:L], ACT.Copy).then_inc(ot_out, 1)

                for slot in range(NB + 4):
                    if slot < NB:
                        a1_exp(slot)
                    if 1 <= slot <= NB:
                        a1_turned(slot - 1)
                    if 3 <= slot <= NB + 2:
                        a1_back(slot - 3)
                layernorm(1)

                def scores(h, t):
                    n = NT * h + t
                    act.wait_ge(sc_mm, n + 1)
                    if n >= 2:
                        act.wait_ge(st_mm, n - 1)
                    A(sc[:, n % 2, :], ps[0:TT, 5, 0:128], ACT.Copy).then_inc(sc_out, 1)

                def partition_sum(h, t):
                    n = NT * h + t
                    act.wait_ge(shift_ready, n + 1)
                    A(cand_e[:, :], top[:, n % 2, 0:TOPK], ACT.Exp, bias=stat[:, n % 2, 1:2],
                      accum_out=stat[:, n % 2, 2:3]).then_inc(z_ready, 1)

                def turned_scores(h, t):
                    n = NT * h + t
                    act.wait_ge(st_mm, n + 1)
                    if h >= 2 and t == 0:
                        act.wait_ge(kv_ready, 2 * h - 2)
                    A(rz_row[:, h % 2, t * TT:(t + 1) * TT], ps[0:128, 5, 256:256 + TT], ACT.Copy)
                    A(st_hi[:, h % 2, t * TT:(t + 1) * TT], ps[0:128, 5, 128:128 + TT], ACT.Copy)\
                        .then_inc(hi_ready, 1)

                def exp_unit(g):
                    act.wait_ge(a_ready, g + 1)
                    if g >= 2:
                        act.wait_ge(w_ready, g - 1)
                    A(halves(expo[:, g % 2, :]), pair(2 * (g % 2), 128), ACT.Exp).then_inc(e_ready, 1)

                def attend(h, u):
                    if u == 0:
                        act.wait_ge(q2_mm, h + 1)
                        A(halves(q2[0:C, :]), pair(6, C), ACT.Copy, scale=SCALE2).then_inc(q2_out, 1)
                    if u == 6:
                        act.wait_ge(s2_sub, h + 1)
                        A(s2[0:L, :], s2[0:L, :], ACT.Exp).then_inc(s2_exp, 1)
                    if u == 10:
                        act.wait_ge(pt2_mm, h + 1)
                        A(halves(pt2[0:L, :]), pair(6, L), ACT.Copy).then_inc(pt2_out, 1)
                    if u == 12:
                        act.wait_ge(v2_mm, h + 1)
                        A(v2[:, :, :].rearrange("p b c -> p (b c)"), ps[0:L, 6, :], ACT.Copy).then_inc(v2_out, 1)
                    if u == 14:
                        act.wait_ge(o2_mm, h + 1)
                        A(halves(o2[0:C, :]), pair(6, C), ACT.Copy).then_inc(o2_out, 1)

                for hh in range(-1, H + 1):
                    for u in range(UNITS):
                        if 0 <= hh < H:
                            exp_unit(hh * UNITS + u)
                        if hh + 1 < H and u % 5 == 0 and u // 5 < NT:
                            scores(hh + 1, u // 5)
                        if hh + 1 < H and u >= 5 and (u - 5) % 5 == 0 and (u - 5) // 5 < NT:
                            partition_sum(hh + 1, (u - 5) // 5)
                        if hh + 1 < H and u >= 6 and (u - 6) % 5 == 0 and (u - 6) // 5 < NT:
                            turned_scores(hh + 1, (u - 6) // 5)
                        if hh >= 1:
                            attend(hh - 1, u)
                act.wait_ge(y_mm, 1)
                act.wait_ge(pt2_mm, H)
                A(y_sb, ps[0:TT, 6, 0:NT * C], ACT.Copy).then_inc(y_out, 1)
                act.drain().then_inc(iter_end, 1)
                act.wait_ge(iter_clear, it + 1)

        @block.vector
        def _(dve):
            V = nc.vector
            V.memset(hid[META:META + 1, :], 1.0).then_inc(set_dve, 1)
            dve.wait_ge(spread_in, 16)
            V.tensor_copy(spread[:, :], spread_f).then_inc(set_dve, 1)
            dve.wait_ge(consts_in, 16 * N_CONSTS)
            V.tensor_scalar(q_scale[:, :], q_scale[:, :], float(np.log(1.0 / 0.01)), None, ALU.min)\
                .then_inc(set_dve, 1)
            dve.wait_ge(set_act, 5)

            with dve.Fori(0, ITERS) as it:
                links = [0]

                def link(ins):
                    ins.then_inc(dve_link, 1)
                    links[0] += 1
                    dve.wait_ge(dve_link, links[0])

                V.tensor_copy(h_sb[:, :].rearrange("p (b n) -> p b n", b=NB)[:, :, 0:1],
                              cls_tok[:, 0:1].unsqueeze(1).to_broadcast([C, NB, 1])).then_inc(cls_set, 1)

                def layernorm(n):
                    dve.wait_ge(std_ready, n + 1)
                    link(V.reciprocal(o2[0:C, :], pt2[0:C, :]))
                    V.tensor_tensor(halves(xh[:, :]), pair(0, C), halves(o2[0:C, :]), ALU.mult)\
                        .then_inc(ln_ready, 1)

                layernorm(0)
                dve.wait_ge(v_mm, 1)
                V.tensor_tensor(v2[:, :, :], ps[0:L, 0, :].rearrange("p (b c) -> p b c", b=NB),
                                b_v[:, :].unsqueeze(1).to_broadcast([L, NB, C]), ALU.add).then_inc(v_out, 1)
                dve.wait_ge(nrm_ready, 1)
                link(V.tensor_scalar(pt2[:, :], pt2[:, :], 1e-12, None, ALU.max))
                link(V.reciprocal(o2[:, :], pt2[:, :]))
                V.scalar_tensor_tensor(out=qn, in0=q2[0:C, :], scalar=q_scale[:, 0:1], in1=o2[0:C, :],
                                       op0=ALU.mult, op1=ALU.mult).then_inc(qk_unit, 1)
                V.tensor_tensor(kn, q2[C:128, :], o2[C:128, :], ALU.mult).then_inc(qk_unit, 1)

                def a1_shift(b):
                    dve.wait_ge(s_mm, b + 1)
                    if b >= 2:
                        dve.wait_ge(pt_mm, b - 1)
                    e = expo[0:L, b % 2, :].rearrange("p (h m) -> p h m", h=H)
                    V.tensor_tensor(halves(expo[0:L, b % 2, :]), pair(2 * (b % 2), L),
                                    halves(pos_bias[:, :, :].rearrange("p h m -> p (h m)")), ALU.add)\
                        .then_inc(s_sub, 1)
                    dve.wait_ge(s_sub, 2 * b + 1)
                    link(V.tensor_reduce(red[:, b % 2, 0:H], e, AX.X, ALU.max))
                    V.tensor_tensor(e, e, red[:, b % 2, 0:H].unsqueeze(2).to_broadcast([L, H, L]), ALU.subtract)\
                        .then_inc(s_sub, 1)

                def a1_sum(b):
                    dve.wait_ge(s_exp, b + 1)
                    e = expo[0:L, b % 2, :].rearrange("p (h m) -> p h m", h=H)
                    link(V.tensor_reduce(red[:, b % 2, H:2 * H], e, AX.X, ALU.add))
                    link(V.reciprocal(red[:, b % 2, H:2 * H], red[:, b % 2, H:2 * H]))

                def a1_scale(b):
                    dve.wait_ge(o_mm, b + 1)
                    if b >= 2:
                        dve.wait_ge(ot_mm, b - 1)
                    V.tensor_tensor(s2[0:L, (b % 2) * C:(b % 2 + 1) * C].rearrange("p (h d) -> p h d", h=H),
                                    ps[0:L, 6, 0:C].rearrange("p (h d) -> p h d", h=H),
                                    red[:, b % 2, H:2 * H].unsqueeze(2).to_broadcast([L, H, HD]), ALU.mult)\
                        .then_inc(o_out, 1)

                for slot in range(NB + 4):
                    if 2 <= slot <= NB + 1:
                        a1_scale(slot - 2)
                    if slot < NB:
                        a1_shift(slot)
                    if 1 <= slot <= NB:
                        a1_sum(slot - 1)
                dve.wait_ge(proj_mm, 1)
                V.scalar_tensor_tensor(out=halves(h_sb[:, :]), in0=pair(0, C), scalar=b_proj[:, 0:1],
                                       in1=halves(h_sb[:, :]), op0=ALU.add, op1=ALU.add).then_inc(h2_ready, 1)
                layernorm(1)

                def best16(h, t, side):
                    n = NT * h + t
                    dve.wait_ge(sc_out, n + 1)
                    s = sc[:, n % 2, side * NK:(side + 1) * NK]
                    link(V.max(best[:, side, 0:8], s))
                    link(V.match_replace(rest[:, 0:NK], best[:, side, 0:8], s, LOWEST))
                    link(V.max(best[:, side, 8:16], rest[:, 0:NK]))

                def candidates(h, t):
                    n = NT * h + t
                    V.tensor_tensor(cand[:, 0:R0 * TOPK].rearrange("p (a b) -> p a b", a=R0),
                                    best[:, 0, 0:R0].unsqueeze(2).to_broadcast([TT, R0, TOPK]),
                                    best[:, 1, :].unsqueeze(1).to_broadcast([TT, R0, TOPK]), ALU.add)
                    link(V.tensor_tensor(cand[:, R0 * TOPK:NCAND].rearrange("p (a b) -> p a b", b=R1),
                                         best[:, 0, R0:TOPK].unsqueeze(2).to_broadcast([TT, TOPK - R0, R1]),
                                         best[:, 1, 0:R1].unsqueeze(1).to_broadcast([TT, TOPK - R0, R1]), ALU.add))
                    link(V.max(top[:, n % 2, 0:8], cand[:, :]))
                    link(V.match_replace(rest[:, :], top[:, n % 2, 0:8], cand[:, :], LOWEST))

                def threshold(h, t):
                    n = NT * h + t
                    tp, st = top[:, n % 2, :], stat[:, n % 2, :]
                    link(V.max(tp[:, 8:16], rest[:, :]))
                    link(V.match_replace(rest[:, :], tp[:, 8:16], rest[:, :], LOWEST))
                    link(V.max(tp[:, 16:24], rest[:, :]))
                    link(V.tensor_scalar(st[:, 0:1], tp[:, 15:16], tp[:, 16:17], -0.5, ALU.add, ALU.mult))
                    link(V.tensor_reduce(st[:, 1:2], best[:, :, :].rearrange("p s k -> p (s k)"), AX.X, ALU.max,
                                         apply_absolute_value=True))
                    link(V.scalar_tensor_tensor(out=st[:, 1:2], in0=st[:, 1:2], scalar=ROUNDING, in1=tp[:, 15:16],
                                                op0=ALU.mult, op1=ALU.subtract))
                    link(V.tensor_scalar(st[:, 0:1], st[:, 1:2], st[:, 0:1], tp[:, 0:1], ALU.min, ALU.add))
                    V.tensor_scalar(st[:, 1:2], st[:, 0:1], EXP_CAP, tp[:, 0:1], ALU.min, ALU.subtract)\
                        .then_inc(shift_ready, 1)
                    dve.wait_ge(shift_ready, n + 1)
                    V.tensor_scalar(sc[:, n % 2, 0:NK], sc[:, n % 2, 0:NK], st[:, 1:2], None, ALU.add)

                def invert_sum(h, t):
                    n = NT * h + t
                    dve.wait_ge(z_ready, n + 1)
                    V.reciprocal(stat[:, n % 2, 3:4], stat[:, n % 2, 2:3]).then_inc(rz_ready, 1)

                def low_part(h, t):
                    n = NT * h + t
                    dve.wait_ge(hi_ready, n + 1)
                    V.tensor_tensor(st_lo[:, h % 2, t * TT:(t + 1) * TT], ps[0:128, 5, 128:128 + TT],
                                    st_hi[:, h % 2, t * TT:(t + 1) * TT].bitcast(F32), ALU.subtract)\
                        .then_inc(st_ready, 1)

                def mask_unit(g):
                    dve.wait_ge(e_ready, g + 1)
                    if g >= 2:
                        dve.wait_ge(out_done, g - 1)
                    V.scalar_tensor_tensor(out=halves(wts[:, g % 2, :]), in0=pair(2 * (g % 2), 128), scalar=0.0,
                                           in1=halves(expo[:, g % 2, :]), op0=ALU.is_ge, op1=ALU.mult)\
                        .then_inc(w_ready, 1)

                def take_sum(k):
                    h, s = k // 2, k % 2
                    dve.wait_ge(out_done, (CH // 2) * (k + 1))
                    V.tensor_tensor(kv[:, h % 2, s * HALF:(s + 1) * HALF], ps[0:128, 4, 0:HALF],
                                    rz_row[:, h % 2, s * HALF:(s + 1) * HALF], ALU.mult).then_inc(kv_ready, 1)

                def attend(h, u):
                    s = s2[0:L, :].rearrange("p (b m) -> p b m", b=NB)
                    if u == 3:
                        dve.wait_ge(s2_mm, h + 1)
                        for k in range(2):
                            last = V.tensor_tensor(
                                s[:, 4 * k:4 * k + 4, :], ps[0:L, 6 + k, 0:HALF].rearrange("p (b m) -> p b m", b=4),
                                causal[:, :].unsqueeze(1).to_broadcast([L, 4, L]), ALU.add)
                        link(last)
                    if u == 4:
                        link(V.tensor_reduce(red[:, 0, 0:NB], s, AX.X, ALU.max))
                    if u == 5:
                        V.tensor_tensor(s, s, red[:, 0, 0:NB].unsqueeze(2).to_broadcast([L, NB, L]), ALU.subtract)\
                            .then_inc(s2_sub, 1)
                    if u == 7:
                        dve.wait_ge(s2_exp, h + 1)
                        link(V.tensor_reduce(red[:, 0, NB:2 * NB], s, AX.X, ALU.add))
                        link(V.reciprocal(red[:, 0, NB:2 * NB], red[:, 0, NB:2 * NB]))
                    if u == 8:
                        V.tensor_tensor(s, s, red[:, 0, NB:2 * NB].unsqueeze(2).to_broadcast([L, NB, L]), ALU.mult)\
                            .then_inc(p2_ready, 1)
                    if u == 17:
                        dve.wait_ge(ffn_mm, h + 1)
                        V.tensor_tensor(halves(h_sb[:, :]), pair(6, C), halves(h_sb[:, :]), ALU.add)\
                            .then_inc(ffn_added, 1)

                for hh in range(-1, H + 1):
                    for u in range(UNITS):
                        g = hh * UNITS + u
                        if 0 <= hh < H:
                            mask_unit(g)
                        if g >= CH // 2 and g % (CH // 2) == 0 and g // (CH // 2) <= 2 * H:
                            take_sum(g // (CH // 2) - 1)
                        if hh + 1 < H:
                            if u >= 7 and (u - 7) % 5 == 0 and (u - 7) // 5 < NT:
                                low_part(hh + 1, (u - 7) // 5)
                            if u >= 5 and (u - 5) % 5 == 0 and (u - 5) // 5 < NT:
                                invert_sum(hh + 1, (u - 5) // 5)
                            if u < 5 * NT:
                                t, step = u // 5, u % 5
                                if step in (1, 2):
                                    best16(hh + 1, t, step - 1)
                                if step == 3:
                                    candidates(hh + 1, t)
                                if step == 4:
                                    threshold(hh + 1, t)
                        if hh >= 1:
                            attend(hh - 1, u)
                dve.drain().then_inc(iter_end, 1)
                dve.wait_ge(iter_clear, it + 1)


def kernel(x, cls_tok, L0_tok_W, L0_tok_b, L0_attn_qkv_w, L0_attn_qkv_b, L0_attn_proj_w, L0_attn_proj_b,
           L0_attn_logit_scale, L0_attn_mlp1_w, L0_attn_mlp1_b, L0_attn_mlp2_w, L0_attn_mlp2_b,
           L0_ffn_Wq_pk, L0_ffn_pk_keys, L0_ffn_Wq, L0_ffn_keys_table, L0_ffn_values_table, L0_ffn_Wo):
    import concourse.bacc as bacc
    from concourse.bass_utils import run_bass_kernel_spmd as run

    a = {k: np.asarray(v) for k, v in locals().items() if k not in ("bacc", "run")}
    f = {k: v.astype(np.float32) for k, v in shape_constants().items()}
    col = lambda v: v.reshape(-1, 1)
    w_tok = np.zeros((4, GRID, GRID, 4, C), np.float32)
    for m, (row, column) in enumerate([(0, 0), (1, 0), (0, 1), (1, 1), (3, 2), (2, 3), (3, 3)]):
        for j in range(GRID):
            w_tok[column, j, j, row] = a["L0_tok_W"][m]
    qkv_w, qkv_b = a["L0_attn_qkv_w"], a["L0_attn_qkv_b"]
    rows = np.concatenate([a["L0_ffn_keys_table"], a["L0_ffn_values_table"]], axis=1)
    f.update({
        "x": a["x"],
        "w_tok": w_tok.reshape(32, -1),
        "tok_b": col(a["L0_tok_b"]), "cls_tok": col(a["cls_tok"]),
        "w_qk": qkv_w[0:2 * C].T, "b_qk": col(qkv_b[0:2 * C]),
        "w_v": qkv_w[2 * C:].T, "b_v": np.broadcast_to(qkv_b[2 * C:], (L, C)),
        "w_proj": a["L0_attn_proj_w"].T, "b_proj": col(a["L0_attn_proj_b"]),
        "q_scale": col(np.repeat(a["L0_attn_logit_scale"], HD)),
        "mlp1": np.concatenate([a["L0_attn_mlp1_w"].T, a["L0_attn_mlp1_b"][None]]),
        "mlp2": np.concatenate([a["L0_attn_mlp2_w"].T, a["L0_attn_mlp2_b"][None]]),
        "w_q2": a["L0_ffn_Wq"],
        "w_o2": a["L0_ffn_Wo"].reshape(H, C, C).transpose(1, 0, 2).reshape(C, H * C),
        "pk_q": a["L0_ffn_Wq_pk"].reshape(C, 2, H, DK).transpose(3, 2, 1, 0).reshape(DK, 2 * H, C),
        "pk_k": a["L0_ffn_pk_keys"].transpose(3, 2, 0, 1).reshape(DK, 2 * H, NK),
        "table": rows.reshape(H, CH, 128, 128).transpose(2, 0, 1, 3).reshape(128, H, CH * 128),
    })
    nc = bacc.Bacc("TRN2", target_bir_lowering=False, num_devices=1)
    arrays, dram = {}, {}
    for name, v in f.items():
        v = np.ascontiguousarray(v)
        arrays[f"in_{name}"] = v
        dram[name] = nc.dram_tensor(f"in_{name}", v.shape, mybir.dt.from_np(v.dtype), kind="ExternalInput").ap()
    dram["out"] = nc.dram_tensor("out", (B, L, C), F32, kind="ExternalOutput").ap()
    build(nc, dram)
    r = run(nc, [arrays], core_ids=[0])
    return r.results[0]["out"]
```

```python
from contextlib import ExitStack

import numpy as np

import concourse.bass as bass
from concourse import mybir

F32 = mybir.dt.float32
F32R = mybir.dt.float32r
ALU = mybir.AluOpType
ACT = mybir.ActivationFunctionType
AX = mybir.AxisListType

B, IMG, C = 64, 112, 64
GRID = 8
L = GRID * GRID + 1
H, HD = 8, 8
META = 96
NK, DK, TOPK = 64, 32, 16
NB = 8
T = NB * L
ITERS = B // NB
HALF = T // 2
TT, NT = T // 5, 5
CH = NK * NK // 128
UNITS = CH
R0 = 4
R1 = 3
NCAND = R0 * TOPK + (TOPK - R0) * R1
LOWEST = -3.0e38
MASKED = -1.0e30
EXP_CAP = 80.0
ROUNDING = 2.0 ** -20
EPS = 1e-5
SCALE2 = float(C) ** -0.5


def shape_constants():
    def resize(n):
        scale = n / GRID
        x = (np.arange(GRID) + 0.5) * scale - 0.5
        w = np.maximum(0.0, 1.0 - np.abs(x[:, None] - np.arange(n)[None, :]) / scale)
        return w / w.sum(axis=1, keepdims=True)

    def haar(n):
        lo, hi = np.zeros((n // 2, n)), np.zeros((n // 2, n))
        i = np.arange(n // 2)
        lo[i, 2 * i] = lo[i, 2 * i + 1] = hi[i, 2 * i] = 0.7071067811865476
        hi[i, 2 * i + 1] = -0.7071067811865476
        return lo, hi

    lo1, hi1 = haar(IMG)
    lo2, hi2 = haar(IMG // 2)
    r1, r2 = resize(IMG // 2), resize(IMG // 4)
    filters = np.concatenate([r2 @ lo2 @ lo1, r2 @ hi2 @ lo1, r1 @ lo1, r1 @ hi1])
    d = np.arange(-(L - 1), L)
    rel = np.stack([0.0 * d, np.sign(d) * np.log1p(np.abs(d)), np.ones(len(d))])
    part = np.arange(128)
    spread = np.zeros((128, CH, 128))
    for c in range(CH):
        spread[part % NK, c, part] = 1.0
        spread[NK + 2 * c + part // NK, c, part] = 1.0
    causal = np.where(np.arange(L)[None, :] <= np.arange(L)[:, None], 0.0, MASKED)
    return {
        "filters": filters.T,
        "rel": rel,
        "spread": spread.reshape(128, CH * 128),
        "ident": np.eye(128),
        "head_sum": np.kron(np.eye(16), np.ones((8, 8))),
        "center": np.eye(C) - 1.0 / C,
        "mean": np.full((C, C), 1.0 / C),
        "head_mask": np.kron(np.eye(H), np.ones((HD, 1))),
        "causal": causal,
    }


def build(nc, d):
    with ExitStack() as ctx:
        def sb(name, shape, dt=F32):
            return ctx.enter_context(nc.sbuf_tensor(name, shape, dt))

        body_sems = []

        def bsem(name):
            s = ctx.enter_context(nc.semaphore(name))
            body_sems.append(s)
            return s

        image_in = bsem("image_in")
        rows_mm, rows_out = bsem("rows_mm"), bsem("rows_out")
        maps_mm, maps_out = bsem("maps_mm"), bsem("maps_out")
        tok_mm, cls_set, h1_ready = bsem("tok_mm"), bsem("cls_set"), bsem("h1_ready")
        cen_mm, sq_ready, var_mm, std_ready, ln_ready = (
            bsem("cen_mm"), bsem("sq_ready"), bsem("var_mm"), bsem("std_ready"), bsem("ln_ready"))
        qk_mm, qk_out, qk_sq, nrm_mm, nrm_ready, qk_unit = (
            bsem("qk_mm"), bsem("qk_out"), bsem("qk_sq"), bsem("nrm_mm"), bsem("nrm_ready"), bsem("qk_unit"))
        v_mm, v_out, kx_ready = bsem("v_mm"), bsem("v_out"), bsem("kx_ready")
        s_mm, s_sub, s_exp, pt_mm, pt_out = (
            bsem("s_mm"), bsem("s_sub"), bsem("s_exp"), bsem("pt_mm"), bsem("pt_out"))
        o_mm, o_out, ot_mm, ot_out, proj_mm, h2_ready = (
            bsem("o_mm"), bsem("o_out"), bsem("ot_mm"), bsem("ot_out"), bsem("proj_mm"), bsem("h2_ready"))
        dve_link = bsem("dve_link")
        sc_mm, sc_out, shift_ready, z_ready, rz_ready, st_mm, hi_ready, st_ready = (
            bsem("sc_mm"), bsem("sc_out"), bsem("shift_ready"), bsem("z_ready"), bsem("rz_ready"),
            bsem("st_mm"), bsem("hi_ready"), bsem("st_ready"))
        pool_link, best_ready, cand_ready, top_ready = (
            bsem("pool_link"), bsem("best_ready"), bsem("cand_ready"), bsem("top_ready"))
        sc_shifted = bsem("sc_shifted")
        s_add, s_red, s2_red, s2_sum = bsem("s_add"), bsem("s_red"), bsem("s2_red"), bsem("s2_sum")
        a_ready, e_ready, w_ready, out_done, kv_ready = (
            bsem("a_ready"), bsem("e_ready"), bsem("w_ready"), bsem("out_done"), bsem("kv_ready"))
        q2_mm, q2_out, s2_mm, s2_sub, s2_exp, p2_ready, pt2_mm, pt2_out = (
            bsem("q2_mm"), bsem("q2_out"), bsem("s2_mm"), bsem("s2_sub"), bsem("s2_exp"),
            bsem("p2_ready"), bsem("pt2_mm"), bsem("pt2_out"))
        v2_mm, v2_out, o2_mm, o2_out, ffn_mm, ffn_added = (
            bsem("v2_mm"), bsem("v2_out"), bsem("o2_mm"), bsem("o2_out"), bsem("ffn_mm"), bsem("ffn_added"))
        y_mm, y_out, y_stored = bsem("y_mm"), bsem("y_out"), bsem("y_stored")

        def sem(name):
            return ctx.enter_context(nc.semaphore(name))

        consts_in, spread_in = sem("consts_in"), sem("spread_in")
        tables_in = [sem(f"table{h}_in") for h in range(H)]
        set_mm, set_act, set_dve = sem("set_mm"), sem("set_act"), sem("set_dve")
        eps_set = sem("eps_set")
        iter_end, iter_clear = sem("iter_end"), sem("iter_clear")

        table = sb("table", [128, H, CH, 128])
        spread = sb("spread", [128, CH * 128], F32R)
        spread_f = table[:, H - 1, :, :].rearrange("p c n -> p (c n)")
        ident = sb("ident", [128, 128])
        filters = sb("filters", [IMG, 32])
        w_tok = sb("w_tok", [128, GRID, C])
        tok_b, cls_tok = sb("tok_b", [C, 1]), sb("cls_tok", [C, 1])
        center, mean = sb("center", [C, C]), sb("mean", [C, C])
        head_sum = sb("head_sum", [128, 128])
        head_mask = sb("head_mask", [C, H])
        w_qk, b_qk = sb("w_qk", [C, 128]), sb("b_qk", [128, 1])
        w_v, b_v = sb("w_v", [C, C]), sb("b_v", [L, C])
        w_proj, b_proj = sb("w_proj", [C, C]), sb("b_proj", [C, 1])
        q_scale = sb("q_scale", [C, 1])
        rel, mlp1, mlp2 = sb("rel", [3, 2 * L - 1]), sb("mlp1", [3, META]), sb("mlp2", [META + 1, H])
        hid = sb("hid", [META + 1, 2 * L - 1])
        pos_bias = sb("pos_bias", [L, H, L])
        causal = sb("causal", [L, L])
        pk_q, pk_k = (table[0:DK, H - 2, 0:8, :].rearrange("p c n -> p (c n)").rearrange("p (g n) -> p g n", g=16),
                      table[0:DK, H - 2, 8:16, :].rearrange("p c n -> p (c n)").rearrange("p (g n) -> p g n", g=16))
        w_sim = sb("w_sim", [C, H, 2 * NK])
        w_q2, w_o2 = sb("w_q2", [C, H * C]), sb("w_o2", [C, H, C])
        eps = sb("eps", [128, 1])

        h_sb, xh = sb("h_sb", [C, T]), sb("xh", [C, T])
        wts = sb("wts", [128, 3, T])
        expo = sb("expo", [128, 2, T])
        kv = sb("kv", [128, 2, T])
        rz_row = sb("rz_row", [128, 2, T])
        st_hi, st_lo = sb("st_hi", [128, 2, T], F32R), sb("st_lo", [128, 2, T], F32R)
        q2, s2, pt2, o2 = sb("q2", [128, T]), sb("s2", [128, T]), sb("pt2", [128, T]), sb("o2", [128, T])
        v2 = sb("v2", [L, NB, C])
        sc = sb("sc", [TT, 4, 2 * NK])
        best = sb("best", [TT, 2, 2, TOPK])
        rest = sb("rest", [TT, 2, NK])
        cand, cand_rest = sb("cand", [TT, NCAND]), sb("cand_rest", [TT, NCAND])
        top = sb("top", [TT, 4, 24])
        stat = sb("stat", [TT, 4, 4])
        cand_e = sb("cand_e", [TT, TOPK])
        red = sb("red", [L, 2, 16])
        image = kv[0:IMG, :, :].rearrange("p a t -> p (a t)")[:, 0:NB * IMG].rearrange("p (b x) -> p b x", b=NB)
        rows = expo[0:IMG, 0, 0:NB * 32]
        maps = expo[:, 1, 0:NB * GRID]
        qn, kn = rz_row[0:C, 0, :], rz_row[0:C, 1, :]
        kx = wts[0:C, 0:2, :].rearrange("p a (h m) -> p a h m", h=H)
        y_sb = s2[0:TT, 0:NT * C]
        ps = ctx.enter_context(nc.psum_tensor("ps", [128, 8, 512], F32))

        def pair(k, parts, n=HALF):
            return ps[0:parts, k:k + 2, 0:n]

        def halves(ap):
            return ap.rearrange("p (s t) -> p s t", s=2)

        def both(eng_mm, bank, parts, lhsT, rhs, sem_):
            for s in range(2):
                mm = eng_mm(ps[0:parts, bank + s, 0:HALF], lhsT, rhs[:, s * HALF:(s + 1) * HALF],
                            start=True, stop=True)
            mm.then_inc(sem_, 1)

        x_v = d["x"].rearrange("b c y x -> y (b c) x")
        out_v = d["out"].rearrange("(i j) n c -> i (j n) c", j=NB).rearrange("i (t p) c -> i p t c", p=TT)

        consts = [(ident, "ident"), (filters, "filters"), (tok_b, "tok_b"), (cls_tok, "cls_tok"),
                  (center, "center"), (mean, "mean"), (head_sum, "head_sum"), (head_mask, "head_mask"),
                  (w_qk, "w_qk"), (b_qk, "b_qk"), (w_v, "w_v"), (b_v, "b_v"), (w_proj, "w_proj"),
                  (b_proj, "b_proj"), (q_scale, "q_scale"), (rel, "rel"), (mlp1, "mlp1"), (mlp2, "mlp2"),
                  (causal, "causal"), (w_q2, "w_q2")]
        N_CONSTS = len(consts) + 4

        def tile_at(u, step):
            t = (u - step) // 4
            return t if (u - step) % 4 == 0 and 0 <= t < NT else None

        block = ctx.enter_context(nc.Block())

        @block.sync
        def _(sp):
            for tile, name in consts:
                sp.dma_start(tile[:, :], d[name]).then_inc(consts_in, 16)
            sp.dma_start(w_tok[:, :, :].rearrange("p j c -> p (j c)"), d["w_tok"]).then_inc(consts_in, 16)
            sp.dma_start(w_o2[:, :, :].rearrange("p h c -> p (h c)"), d["w_o2"]).then_inc(consts_in, 16)
            sp.dma_start(pk_q, d["pk_q"]).then_inc(consts_in, 16)
            sp.dma_start(pk_k, d["pk_k"]).then_inc(consts_in, 16)
            sp.dma_start(spread_f, d["spread"]).then_inc(spread_in, 16)
            for h in range(H - 2):
                sp.dma_start(table[:, h, :, :].rearrange("p c n -> p (c n)"), d["table"][:, h, :])\
                  .then_inc(tables_in[h], 16)
            sp.wait_ge(consts_in, 16 * N_CONSTS)
            sp.wait_ge(spread_in, 16)
            sp.wait_ge(set_mm, 2)
            sp.wait_ge(set_dve, 2)
            for h in range(H - 2, H):
                sp.dma_start(table[:, h, :, :].rearrange("p c n -> p (c n)"), d["table"][:, h, :])\
                  .then_inc(tables_in[h], 16)
            with sp.Fori(0, ITERS) as it:
                sp.dma_start(image, x_v[:, bass.ds(it * NB, NB), :]).then_inc(image_in, 16)
                sp.wait_ge(y_out, 1)
                sp.dma_start(out_v[bass.ds(it, 1), :, :, :].rearrange("i p t c -> (i p) t c"),
                             y_sb.rearrange("p (t c) -> p t c", t=NT)).then_inc(y_stored, 16)
                sp.wait_ge(y_stored, 16)
                sp.drain().then_inc(iter_end, 1)
                sp.wait_ge(iter_clear, it + 1)
                sp.nop(nofuse=True)

        @block.gpsimd
        def _(pool):
            nc.gpsimd.memset(eps[:, :], EPS).then_inc(eps_set, 1)
            pool.wait_ge(consts_in, 16 * N_CONSTS)
            with pool.Fori(0, ITERS) as it:
                links = [0]

                def link(ins):
                    ins.then_inc(pool_link, 1)
                    links[0] += 1
                    pool.wait_ge(pool_link, links[0])

                P = nc.gpsimd

                def spread_keys(b):
                    pool.wait_ge(qk_unit, 2)
                    if b >= 2:
                        pool.wait_ge(s_mm, b - 1)
                    P.tensor_tensor(kx[:, b % 2, :, :],
                                    kn[:, b * L:(b + 1) * L].unsqueeze(1).to_broadcast([C, H, L]),
                                    head_mask[:, :].unsqueeze(2).to_broadcast([C, H, L]), ALU.mult)\
                        .then_inc(kx_ready, 1)

                def a1_shift(b):
                    pool.wait_ge(s_red, b + 1)
                    e = expo[0:L, b % 2, :].rearrange("p (h m) -> p h m", h=H)
                    P.tensor_tensor(e, e, red[:, b % 2, 0:H].unsqueeze(2).to_broadcast([L, H, L]), ALU.subtract)\
                        .then_inc(s_sub, 1)

                for b in range(NB + 1):
                    if b < NB:
                        spread_keys(b)
                    if b >= 1:
                        a1_shift(b - 1)

                def candidates(h, t):
                    n = NT * h + t
                    pool.wait_ge(best_ready, 6 * (n + 1))
                    if n >= 1:
                        pool.wait_ge(top_ready, 5 * (n - 1) + 2)
                    b0, b1 = best[:, n % 2, 0, :], best[:, n % 2, 1, :]
                    P.tensor_tensor(cand[:, 0:R0 * TOPK].rearrange("p (a b) -> p a b", a=R0),
                                    b0[:, 0:R0].unsqueeze(2).to_broadcast([TT, R0, TOPK]),
                                    b1.unsqueeze(1).to_broadcast([TT, R0, TOPK]), ALU.add)
                    P.tensor_tensor(cand[:, R0 * TOPK:NCAND].rearrange("p (a b) -> p a b", b=R1),
                                    b0[:, R0:TOPK].unsqueeze(2).to_broadcast([TT, TOPK - R0, R1]),
                                    b1[:, 0:R1].unsqueeze(1).to_broadcast([TT, TOPK - R0, R1]), ALU.add)\
                        .then_inc(cand_ready, 1)

                def threshold(h, t):
                    n = NT * h + t
                    tp, st = top[:, n % 4, :], stat[:, n % 4, :]
                    pool.wait_ge(top_ready, 5 * (n + 1))
                    P.tensor_scalar(st[:, 1:2], tp[:, 15:16], tp[:, 16:17], -0.5, ALU.add, ALU.mult)
                    link(P.tensor_scalar(st[:, 0:1], st[:, 0:1], ROUNDING, tp[:, 15:16], ALU.mult, ALU.subtract))
                    link(P.tensor_scalar(st[:, 0:1], st[:, 0:1], st[:, 1:2], tp[:, 0:1], ALU.min, ALU.add))
                    P.tensor_scalar(st[:, 1:2], st[:, 0:1], EXP_CAP, tp[:, 0:1], ALU.min, ALU.subtract)\
                        .then_inc(shift_ready, 1)
                    pool.wait_ge(shift_ready, n + 1)
                    P.tensor_scalar(sc[:, n % 4, 0:NK], sc[:, n % 4, 0:NK], st[:, 1:2], None, ALU.add)\
                        .then_inc(sc_shifted, 1)

                def attend(h, u):
                    s = s2[0:L, :].rearrange("p (b m) -> p b m", b=NB)
                    if u == 5:
                        pool.wait_ge(s2_red, h + 1)
                        P.tensor_tensor(s, s, red[:, 0, 0:NB].unsqueeze(2).to_broadcast([L, NB, L]), ALU.subtract)\
                            .then_inc(s2_sub, 1)
                    if u == 10:
                        pool.wait_ge(s2_sum, h + 1)
                        P.tensor_tensor(s, s, red[:, 0, NB:2 * NB].unsqueeze(2).to_broadcast([L, NB, L]), ALU.mult)\
                            .then_inc(p2_ready, 1)

                for hh in range(-1, H + 1):
                    for u in range(UNITS):
                        if hh + 1 < H and tile_at(u, 4) is not None:
                            candidates(hh + 1, tile_at(u, 4))
                        if hh + 1 < H and tile_at(u, 10) is not None:
                            threshold(hh + 1, tile_at(u, 10))
                        if hh >= 1:
                            attend(hh - 1, u)
                pool.wait_ge(iter_end, it * 4 + 4)
                pool.nop(nofuse=True)
                for s in body_sems:
                    pool.sem_clear(s)
                pool.nop().then_inc(iter_clear, 1)

        @block.tensor
        def _(pe):
            mm = nc.tensor.matmul
            tr = nc.tensor.transpose
            pe.wait_ge(consts_in, 16 * N_CONSTS)
            mm(ps[0:META, 0, 0:2 * L - 1], mlp1[:, :], rel[:, :], start=True, stop=True).then_inc(set_mm, 1)
            for g in range(2 * H):
                last = mm(ps[0:C, 2 + g // 8, (g % 8) * NK:(g % 8 + 1) * NK], pk_q[:, g, :], pk_k[:, g, :],
                          start=True, stop=True)
            last.then_inc(set_mm, 1)
            pe.wait_ge(set_act, 1)
            pe.wait_ge(set_dve, 1)
            for m in range(L):
                last = mm(ps[0:L, 4 + m // NK, (m % NK) * H:(m % NK + 1) * H], hid[:, L - 1 - m:2 * L - 1 - m],
                          mlp2[:, :], start=True, stop=True)
            last.then_inc(set_mm, 1)
            pe.wait_ge(set_act, 4)

            with pe.Fori(0, ITERS) as it:
                pe.wait_ge(image_in, 16)
                for b in range(NB):
                    last = mm(ps[0:IMG, 6, b * 32:(b + 1) * 32], image[:, b, :], filters[:, :], start=True, stop=True)
                last.then_inc(rows_mm, 1)
                pe.wait_ge(rows_out, 1)
                rows_v = rows.rearrange("p (b r i) -> p b r i", b=NB, r=4)
                for r in range(4):
                    last = mm(ps[32 * r:32 * r + 32, 7, 0:NB * GRID], filters[:, :], rows_v[:, :, r, :],
                              start=True, stop=True)
                last.then_inc(maps_mm, 1)
                pe.wait_ge(maps_out, 1)
                for j in range(GRID):
                    last = mm(ps[0:C, 6, j * 64:(j + 1) * 64], w_tok[:, j, :], maps, start=True, stop=True)
                last.then_inc(tok_mm, 1)

                def layernorm(n):
                    if n == 0:
                        pe.wait_ge(h1_ready, 1)
                        pe.wait_ge(cls_set, 1)
                    else:
                        pe.wait_ge(h2_ready, 1)
                    both(mm, 0, C, center[:, :], h_sb[:, :], cen_mm)
                    pe.wait_ge(sq_ready, n + 1)
                    both(mm, 2, C, mean[:, :], s2[0:C, :], var_mm)

                layernorm(0)
                pe.wait_ge(ln_ready, 1)
                both(mm, 4, 128, w_qk[:, :], xh[:, :], qk_mm)
                for b in range(NB):
                    last = mm(ps[0:L, 0, b * C:(b + 1) * C], xh[:, b * L:(b + 1) * L], w_v[:, :],
                              start=True, stop=True)
                last.then_inc(v_mm, 1)
                pe.wait_ge(qk_sq, 1)
                both(mm, 6, 128, head_sum[:, :], s2[:, :], nrm_mm)

                def a1_scores(b):
                    pe.wait_ge(kx_ready, b + 1)
                    if b == 0:
                        pe.wait_ge(v_out, 1)
                    if b >= 2:
                        pe.wait_ge(s_add, b - 1)
                    bank = 2 * (b % 2)
                    for s in range(2):
                        last = mm(ps[0:L, bank + s, 0:HALF], qn[:, b * L:(b + 1) * L],
                                  kx[:, b % 2, 4 * s:4 * s + 4, :].rearrange("p h m -> p (h m)"), start=True, stop=True)
                    last.then_inc(s_mm, 1)

                def a1_turn(b):
                    pe.wait_ge(s_exp, b + 1)
                    if b >= 1:
                        pe.wait_ge(pt_out, b)
                    e = expo[0:L, b % 2, :].rearrange("p (h m) -> p h m", h=H)
                    for h in range(H):
                        last = tr(ps[0:L, 4 + h // 4, (h % 4) * L:(h % 4 + 1) * L], e[:, h, :], ident[0:L, 0:L])
                    last.then_inc(pt_mm, 1)

                def a1_values(b):
                    pe.wait_ge(pt_out, b + 1)
                    if b >= 1:
                        pe.wait_ge(o_out, b)
                    pt = kv[0:L, b % 2, :].rearrange("p (h l) -> p h l", h=H)
                    for h in range(H):
                        last = mm(ps[0:L, 6, h * HD:(h + 1) * HD], pt[:, h, :], v2[:, b, h * HD:(h + 1) * HD],
                                  start=True, stop=True)
                    last.then_inc(o_mm, 1)

                def a1_back(b):
                    pe.wait_ge(o_out, b + 1)
                    if b >= 1:
                        pe.wait_ge(ot_out, b)
                    tr(ps[0:C, 7, 0:L], s2[0:L, (b % 2) * C:(b % 2 + 1) * C], ident[0:L, 0:L]).then_inc(ot_mm, 1)

                pe.wait_ge(nrm_ready, 1)
                for slot in range(NB + 4):
                    if slot < NB:
                        a1_scores(slot)
                    if 1 <= slot <= NB:
                        a1_turn(slot - 1)
                    if 2 <= slot <= NB + 1:
                        a1_values(slot - 2)
                    if 3 <= slot <= NB + 2:
                        a1_back(slot - 3)
                pe.wait_ge(ot_out, NB)
                both(mm, 0, C, w_proj[:, :], o2[0:C, :], proj_mm)
                layernorm(1)
                pe.wait_ge(ln_ready, 2)

                def scores(h, t):
                    n = NT * h + t
                    if n >= 1:
                        pe.wait_ge(sc_out, n)
                        pe.wait_ge(st_ready, NT * h + max(0, t - 3))
                    mm(ps[0:TT, 5, 0:128], xh[:, t * TT:(t + 1) * TT], w_sim[:, h, :],
                       start=True, stop=True).then_inc(sc_mm, 1)

                def turn_scores(h, t):
                    n = NT * h + t
                    pe.wait_ge(sc_shifted, n + 1)
                    pe.wait_ge(rz_ready, n + 1)
                    pe.wait_ge(sc_out, NT * h + min(t + 4, NT))
                    pe.wait_ge(st_ready, n)
                    tr(ps[0:128, 5, 128:128 + TT], sc[:, n % 4, :], ident[0:TT, 0:TT])
                    mm(ps[0:128, 5, 256:256 + TT], stat[:, n % 4, 3:4].to_broadcast([TT, 128]), ident[0:TT, 0:TT],
                       start=True, stop=True).then_inc(st_mm, 1)

                def spread_scores(g):
                    h, u = g // UNITS, g % UNITS
                    s, cp = u // (CH // 2), u % (CH // 2)
                    if u == 0:
                        pe.wait_ge(st_ready, NT * (h + 1))
                    if g >= 2:
                        pe.wait_ge(w_ready, g - 1)
                    for k in range(2):
                        w = spread[:, (2 * cp + k) * 128:(2 * cp + k + 1) * 128]
                        o = ps[0:128, 2 * (g % 2) + k, 0:HALF]
                        mm(o, w, st_hi[:, h % 2, s * HALF:(s + 1) * HALF], start=True, stop=False)
                        last = mm(o, w, st_lo[:, h % 2, s * HALF:(s + 1) * HALF], start=False, stop=True)
                    last.then_inc(a_ready, 1)

                def add_rows(g):
                    h, u = g // UNITS, g % UNITS
                    cp = u % (CH // 2)
                    pe.wait_ge(w_ready, g + 1)
                    pe.wait_ge(tables_in[h], 16)
                    if cp == 0 and g > 0:
                        pe.wait_ge(kv_ready, g // (CH // 2))
                    for k in range(2):
                        last = mm(ps[0:128, 4, 0:HALF], table[:, h, 2 * cp + k, :],
                                  wts[:, g % 3, k * HALF:(k + 1) * HALF],
                                  start=(cp == 0 and k == 0), stop=(cp == CH // 2 - 1 and k == 1))
                    last.then_inc(out_done, 1)

                def attend(h, u):
                    if u == 0:
                        if h > 0:
                            pe.wait_ge(ffn_added, h)
                        both(mm, 6, C, w_q2[:, h * C:(h + 1) * C], xh[:, :], q2_mm)
                    if u == 2:
                        pe.wait_ge(q2_out, h + 1)
                        pe.wait_ge(kv_ready, 2 * h + 2)
                        for b in range(NB):
                            last = mm(ps[0:L, 6 + b // 4, (b % 4) * L:(b % 4 + 1) * L], q2[0:C, b * L:(b + 1) * L],
                                      kv[0:C, h % 2, b * L:(b + 1) * L], start=True, stop=True)
                        last.then_inc(s2_mm, 1)
                    if u == 12:
                        pe.wait_ge(p2_ready, h + 1)
                        for b in range(NB):
                            last = tr(ps[0:L, 6 + b // 4, (b % 4) * L:(b % 4 + 1) * L],
                                      s2[0:L, b * L:(b + 1) * L], ident[0:L, 0:L])
                        last.then_inc(pt2_mm, 1)
                    if u == 14:
                        pe.wait_ge(pt2_out, h + 1)
                        for b in range(NB):
                            last = tr(ps[0:L, 6, b * C:(b + 1) * C], kv[C:128, h % 2, b * L:(b + 1) * L],
                                      ident[C:128, C:128])
                        last.then_inc(v2_mm, 1)
                    if u == 16:
                        pe.wait_ge(v2_out, h + 1)
                        for b in range(NB):
                            last = mm(ps[0:C, 6 + b // 4, (b % 4) * L:(b % 4 + 1) * L], v2[:, b, :],
                                      pt2[0:L, b * L:(b + 1) * L], start=True, stop=True)
                        last.then_inc(o2_mm, 1)
                    if u == 18:
                        pe.wait_ge(o2_out, h + 1)
                        both(mm, 6, C, w_o2[:, h, :], o2[0:C, :], ffn_mm)

                for hh in range(-1, H + 1):
                    for u in range(UNITS):
                        g = hh * UNITS + u
                        if 0 <= g + 1 < H * UNITS:
                            spread_scores(g + 1)
                        if 0 <= g - 1 < H * UNITS:
                            add_rows(g - 1)
                        if hh + 1 < H and tile_at(u, 0) is not None:
                            scores(hh + 1, tile_at(u, 0))
                        if hh + 1 < H and tile_at(u, 12) is not None:
                            turn_scores(hh + 1, tile_at(u, 12))
                        if hh >= 1:
                            attend(hh - 1, u)
                pe.wait_ge(ffn_added, H)
                for t in range(NT):
                    last = tr(ps[0:TT, 6, t * C:(t + 1) * C], h_sb[:, t * TT:(t + 1) * TT], ident[0:C, 0:C])
                last.then_inc(y_mm, 1)
                pe.drain().then_inc(iter_end, 1)
                pe.wait_ge(iter_clear, it + 1)

        @block.scalar
        def _(act):
            A = nc.scalar.activation
            act.wait_ge(set_mm, 1)
            A(hid[0:META, :], ps[0:META, 0, 0:2 * L - 1], ACT.Relu).then_inc(set_act, 1)
            act.wait_ge(set_mm, 2)
            A(w_sim[:, :, :].rearrange("p h n -> p (h n)"),
              ps[0:C, 2:4, :].rearrange("p a n -> p (a n)"), ACT.Copy).then_inc(set_act, 1)
            act.wait_ge(set_mm, 3)
            A(pos_bias[:, :, 0:NK], ps[0:L, 4, :].rearrange("p (m h) -> p h m", h=H), ACT.Copy)\
                .then_inc(set_act, 1)
            A(pos_bias[:, :, NK:L], ps[0:L, 5, 0:H].rearrange("p (m h) -> p h m", h=H), ACT.Copy)\
                .then_inc(set_act, 1)
            act.wait_ge(set_dve, 3)
            A(q_scale[:, :], q_scale[:, :], ACT.Exp).then_inc(set_act, 1)

            with act.Fori(0, ITERS) as it:
                act.wait_ge(rows_mm, 1)
                A(rows, ps[0:IMG, 6, 0:NB * 32], ACT.Copy).then_inc(rows_out, 1)
                act.wait_ge(maps_mm, 1)
                A(maps, ps[0:128, 7, 0:NB * GRID], ACT.Copy).then_inc(maps_out, 1)
                act.wait_ge(tok_mm, 1)
                h_tok = h_sb[:, :].rearrange("p (b n) -> p b n", b=NB)[:, :, 1:L]\
                    .rearrange("p b (i j) -> p j b i", j=GRID)
                tok = ps[0:C, 6, :].rearrange("p (j b i) -> p j b i", j=GRID, b=NB)
                for j in range(GRID):
                    last = A(h_tok[:, j, :, :], tok[:, j, :, :], ACT.Identity, bias=tok_b[:, 0:1])
                last.then_inc(h1_ready, 1)

                def layernorm(n):
                    act.wait_ge(cen_mm, n + 1)
                    A(halves(s2[0:C, :]), pair(0, C), ACT.Square).then_inc(sq_ready, 1)
                    act.wait_ge(eps_set, 1)
                    act.wait_ge(var_mm, n + 1)
                    A(halves(pt2[0:C, :]), pair(2, C), ACT.Sqrt, bias=eps[0:C, 0:1]).then_inc(std_ready, 1)

                layernorm(0)
                act.wait_ge(qk_mm, 1)
                A(halves(q2[:, :]), pair(4, 128), ACT.Identity, bias=b_qk[:, 0:1]).then_inc(qk_out, 1)
                act.wait_ge(qk_out, 1)
                A(s2[:, :], q2[:, :], ACT.Square).then_inc(qk_sq, 1)
                act.wait_ge(nrm_mm, 1)
                act.wait_ge(ln_ready, 1)
                A(halves(pt2[:, :]), pair(6, 128), ACT.Sqrt).then_inc(nrm_ready, 1)

                def a1_exp(b):
                    act.wait_ge(s_sub, b + 1)
                    A(expo[0:L, b % 2, :], expo[0:L, b % 2, :], ACT.Exp).then_inc(s_exp, 1)

                def a1_turned(b):
                    act.wait_ge(pt_mm, b + 1)
                    if b >= 2:
                        act.wait_ge(o_mm, b - 1)
                    A(halves(kv[0:L, b % 2, :]), pair(4, L), ACT.Copy).then_inc(pt_out, 1)

                def a1_back(b):
                    act.wait_ge(ot_mm, b + 1)
                    A(o2[0:C, b * L:(b + 1) * L], ps[0:C, 7, 0:L], ACT.Copy).then_inc(ot_out, 1)

                for slot in range(NB + 4):
                    if slot < NB:
                        a1_exp(slot)
                    if 1 <= slot <= NB:
                        a1_turned(slot - 1)
                    if 3 <= slot <= NB + 2:
                        a1_back(slot - 3)
                layernorm(1)

                def scores(h, t):
                    n = NT * h + t
                    act.wait_ge(sc_mm, n + 1)
                    if n >= 4:
                        act.wait_ge(st_mm, n - 3)
                    A(sc[:, n % 4, :], ps[0:TT, 5, 0:128], ACT.Copy).then_inc(sc_out, 1)

                def partition_sum(h, t):
                    n = NT * h + t
                    act.wait_ge(shift_ready, n + 1)
                    A(cand_e[:, :], top[:, n % 4, 0:TOPK], ACT.Exp, bias=stat[:, n % 4, 1:2],
                      accum_out=stat[:, n % 4, 2:3]).then_inc(z_ready, 1)

                def turned_scores(h, t):
                    n = NT * h + t
                    act.wait_ge(st_mm, n + 1)
                    if h >= 2 and t == 0:
                        act.wait_ge(kv_ready, 2 * h - 2)
                    A(rz_row[:, h % 2, t * TT:(t + 1) * TT], ps[0:128, 5, 256:256 + TT], ACT.Copy)
                    A(st_hi[:, h % 2, t * TT:(t + 1) * TT], ps[0:128, 5, 128:128 + TT], ACT.Copy)\
                        .then_inc(hi_ready, 1)

                def exp_unit(g):
                    act.wait_ge(a_ready, g + 1)
                    if g >= 3:
                        act.wait_ge(out_done, g - 2)
                    A(halves(wts[:, g % 3, :]), pair(2 * (g % 2), 128), ACT.Exp).then_inc(e_ready, 1)

                def attend(h, u):
                    if u == 0:
                        act.wait_ge(q2_mm, h + 1)
                        A(halves(q2[0:C, :]), pair(6, C), ACT.Copy, scale=SCALE2).then_inc(q2_out, 1)
                    if u == 7:
                        act.wait_ge(s2_sub, h + 1)
                        A(s2[0:L, :], s2[0:L, :], ACT.Exp).then_inc(s2_exp, 1)
                    if u == 12:
                        act.wait_ge(pt2_mm, h + 1)
                        A(halves(pt2[0:L, :]), pair(6, L), ACT.Copy).then_inc(pt2_out, 1)
                    if u == 14:
                        act.wait_ge(v2_mm, h + 1)
                        A(v2[:, :, :].rearrange("p b c -> p (b c)"), ps[0:L, 6, :], ACT.Copy).then_inc(v2_out, 1)
                    if u == 16:
                        act.wait_ge(o2_mm, h + 1)
                        A(halves(o2[0:C, :]), pair(6, C), ACT.Copy).then_inc(o2_out, 1)

                for hh in range(-1, H + 1):
                    for u in range(UNITS):
                        if 0 <= hh < H:
                            exp_unit(hh * UNITS + u)
                        if hh + 1 < H and tile_at(u, 0) is not None:
                            scores(hh + 1, tile_at(u, 0))
                        if hh + 1 < H and tile_at(u, 11) is not None:
                            partition_sum(hh + 1, tile_at(u, 11))
                        if hh + 1 < H and tile_at(u, 12) is not None:
                            turned_scores(hh + 1, tile_at(u, 12))
                        if hh >= 1:
                            attend(hh - 1, u)
                act.wait_ge(y_mm, 1)
                act.wait_ge(pt2_mm, H)
                A(y_sb, ps[0:TT, 6, 0:NT * C], ACT.Copy).then_inc(y_out, 1)
                act.drain().then_inc(iter_end, 1)
                act.wait_ge(iter_clear, it + 1)

        @block.vector
        def _(dve):
            V = nc.vector
            V.memset(hid[META:META + 1, :], 1.0).then_inc(set_dve, 1)
            dve.wait_ge(spread_in, 16)
            V.tensor_copy(spread[:, :], spread_f).then_inc(set_dve, 1)
            dve.wait_ge(consts_in, 16 * N_CONSTS)
            V.tensor_scalar(q_scale[:, :], q_scale[:, :], float(np.log(1.0 / 0.01)), None, ALU.min)\
                .then_inc(set_dve, 1)
            dve.wait_ge(set_act, 5)

            with dve.Fori(0, ITERS) as it:
                links = [0]

                def link(ins):
                    ins.then_inc(dve_link, 1)
                    links[0] += 1
                    dve.wait_ge(dve_link, links[0])

                V.tensor_copy(h_sb[:, :].rearrange("p (b n) -> p b n", b=NB)[:, :, 0:1],
                              cls_tok[:, 0:1].unsqueeze(1).to_broadcast([C, NB, 1])).then_inc(cls_set, 1)

                def layernorm(n):
                    dve.wait_ge(std_ready, n + 1)
                    link(V.reciprocal(o2[0:C, :], pt2[0:C, :]))
                    V.tensor_tensor(halves(xh[:, :]), pair(0, C), halves(o2[0:C, :]), ALU.mult)\
                        .then_inc(ln_ready, 1)

                layernorm(0)
                dve.wait_ge(v_mm, 1)
                V.tensor_tensor(v2[:, :, :], ps[0:L, 0, :].rearrange("p (b c) -> p b c", b=NB),
                                b_v[:, :].unsqueeze(1).to_broadcast([L, NB, C]), ALU.add).then_inc(v_out, 1)
                dve.wait_ge(nrm_ready, 1)
                link(V.tensor_scalar(pt2[:, :], pt2[:, :], 1e-12, None, ALU.max))
                link(V.reciprocal(o2[:, :], pt2[:, :]))
                V.scalar_tensor_tensor(out=qn, in0=q2[0:C, :], scalar=q_scale[:, 0:1], in1=o2[0:C, :],
                                       op0=ALU.mult, op1=ALU.mult).then_inc(qk_unit, 1)
                V.tensor_tensor(kn, q2[C:128, :], o2[C:128, :], ALU.mult).then_inc(qk_unit, 1)

                def a1_shift(b):
                    dve.wait_ge(s_mm, b + 1)
                    if b >= 2:
                        dve.wait_ge(pt_mm, b - 1)
                    e = expo[0:L, b % 2, :].rearrange("p (h m) -> p h m", h=H)
                    V.tensor_tensor(halves(expo[0:L, b % 2, :]), pair(2 * (b % 2), L),
                                    halves(pos_bias[:, :, :].rearrange("p h m -> p (h m)")), ALU.add)\
                        .then_inc(s_add, 1)
                    dve.wait_ge(s_add, b + 1)
                    V.tensor_reduce(red[:, b % 2, 0:H], e, AX.X, ALU.max).then_inc(s_red, 1)

                def a1_sum(b):
                    dve.wait_ge(s_exp, b + 1)
                    e = expo[0:L, b % 2, :].rearrange("p (h m) -> p h m", h=H)
                    link(V.tensor_reduce(red[:, b % 2, H:2 * H], e, AX.X, ALU.add))
                    link(V.reciprocal(red[:, b % 2, H:2 * H], red[:, b % 2, H:2 * H]))

                def a1_scale(b):
                    dve.wait_ge(o_mm, b + 1)
                    if b >= 2:
                        dve.wait_ge(ot_mm, b - 1)
                    V.tensor_tensor(s2[0:L, (b % 2) * C:(b % 2 + 1) * C].rearrange("p (h d) -> p h d", h=H),
                                    ps[0:L, 6, 0:C].rearrange("p (h d) -> p h d", h=H),
                                    red[:, b % 2, H:2 * H].unsqueeze(2).to_broadcast([L, H, HD]), ALU.mult)\
                        .then_inc(o_out, 1)

                for slot in range(NB + 4):
                    if 2 <= slot <= NB + 1:
                        a1_scale(slot - 2)
                    if slot < NB:
                        a1_shift(slot)
                    if 1 <= slot <= NB:
                        a1_sum(slot - 1)
                dve.wait_ge(proj_mm, 1)
                V.scalar_tensor_tensor(out=halves(h_sb[:, :]), in0=pair(0, C), scalar=b_proj[:, 0:1],
                                       in1=halves(h_sb[:, :]), op0=ALU.add, op1=ALU.add).then_inc(h2_ready, 1)
                layernorm(1)

                def best16(h, t, step):
                    n = NT * h + t
                    if step == 1:
                        dve.wait_ge(sc_out, n + 1)
                        if n >= 2:
                            dve.wait_ge(cand_ready, n - 1)
                    else:
                        dve.wait_ge(best_ready, 6 * n + 2 * (step - 1))
                    for side in range(2):
                        s = sc[:, n % 4, side * NK:(side + 1) * NK]
                        top8 = best[:, n % 2, side, 0:8]
                        if step == 1:
                            V.max(top8, s).then_inc(best_ready, 1)
                        if step == 2:
                            V.match_replace(rest[:, side, :], top8, s, LOWEST).then_inc(best_ready, 1)
                        if step == 3:
                            V.max(best[:, n % 2, side, 8:16], rest[:, side, :]).then_inc(best_ready, 1)

                def top24(h, t, step):
                    n = NT * h + t
                    if step == 0:
                        dve.wait_ge(cand_ready, n + 1)
                        if n >= 4:
                            dve.wait_ge(st_mm, n - 3)
                        V.tensor_reduce(stat[:, n % 4, 0:1], best[:, n % 2, :, :].rearrange("p s k -> p (s k)"),
                                        AX.X, ALU.max, apply_absolute_value=True)
                    else:
                        dve.wait_ge(top_ready, 5 * n + step)
                    k = step // 2
                    src = cand[:, :] if step < 2 else cand_rest[:, :]
                    if step % 2 == 0:
                        V.max(top[:, n % 4, 8 * k:8 * k + 8], src).then_inc(top_ready, 1)
                    else:
                        V.match_replace(cand_rest[:, :], top[:, n % 4, 8 * k:8 * k + 8], src, LOWEST)\
                            .then_inc(top_ready, 1)

                def invert_sum(h, t):
                    n = NT * h + t
                    dve.wait_ge(z_ready, n + 1)
                    V.reciprocal(stat[:, n % 4, 3:4], stat[:, n % 4, 2:3]).then_inc(rz_ready, 1)

                def low_part(h, t):
                    n = NT * h + t
                    dve.wait_ge(hi_ready, n + 1)
                    V.tensor_tensor(st_lo[:, h % 2, t * TT:(t + 1) * TT], ps[0:128, 5, 128:128 + TT],
                                    st_hi[:, h % 2, t * TT:(t + 1) * TT].bitcast(F32), ALU.subtract)\
                        .then_inc(st_ready, 1)

                def mask_unit(g):
                    dve.wait_ge(e_ready, g + 1)
                    V.scalar_tensor_tensor(out=halves(wts[:, g % 3, :]), in0=pair(2 * (g % 2), 128), scalar=0.0,
                                           in1=halves(wts[:, g % 3, :]), op0=ALU.is_ge, op1=ALU.mult)\
                        .then_inc(w_ready, 1)

                def take_sum(k):
                    h, s = k // 2, k % 2
                    dve.wait_ge(out_done, (CH // 2) * (k + 1))
                    V.tensor_tensor(kv[:, h % 2, s * HALF:(s + 1) * HALF], ps[0:128, 4, 0:HALF],
                                    rz_row[:, h % 2, s * HALF:(s + 1) * HALF], ALU.mult).then_inc(kv_ready, 1)

                def attend(h, u):
                    s = s2[0:L, :].rearrange("p (b m) -> p b m", b=NB)
                    if u == 3:
                        dve.wait_ge(s2_mm, h + 1)
                        for k in range(2):
                            last = V.tensor_tensor(
                                s[:, 4 * k:4 * k + 4, :], ps[0:L, 6 + k, 0:HALF].rearrange("p (b m) -> p b m", b=4),
                                causal[:, :].unsqueeze(1).to_broadcast([L, 4, L]), ALU.add)
                        link(last)
                    if u == 4:
                        V.tensor_reduce(red[:, 0, 0:NB], s, AX.X, ALU.max).then_inc(s2_red, 1)
                    if u == 8:
                        dve.wait_ge(s2_exp, h + 1)
                        link(V.tensor_reduce(red[:, 0, NB:2 * NB], s, AX.X, ALU.add))
                    if u == 9:
                        V.reciprocal(red[:, 0, NB:2 * NB], red[:, 0, NB:2 * NB]).then_inc(s2_sum, 1)
                    if u == 19:
                        dve.wait_ge(ffn_mm, h + 1)
                        V.tensor_tensor(halves(h_sb[:, :]), pair(6, C), halves(h_sb[:, :]), ALU.add)\
                            .then_inc(ffn_added, 1)

                for hh in range(-1, H + 1):
                    for u in range(UNITS):
                        g = hh * UNITS + u
                        if 0 <= hh < H:
                            mask_unit(g)
                        if g >= CH // 2 and g % (CH // 2) == 0 and g // (CH // 2) <= 2 * H:
                            take_sum(g // (CH // 2) - 1)
                        if hh + 1 < H:
                            if tile_at(u, 13) is not None:
                                low_part(hh + 1, tile_at(u, 13))
                            if tile_at(u, 11) is not None:
                                invert_sum(hh + 1, tile_at(u, 11))
                            for step in reversed(range(5)):
                                if tile_at(u, 5 + step) is not None:
                                    top24(hh + 1, tile_at(u, 5 + step), step)
                            for step in (1, 2, 3):
                                if tile_at(u, step) is not None:
                                    best16(hh + 1, tile_at(u, step), step)
                        if hh >= 1:
                            attend(hh - 1, u)
                dve.drain().then_inc(iter_end, 1)
                dve.wait_ge(iter_clear, it + 1)


def kernel(x, cls_tok, L0_tok_W, L0_tok_b, L0_attn_qkv_w, L0_attn_qkv_b, L0_attn_proj_w, L0_attn_proj_b,
           L0_attn_logit_scale, L0_attn_mlp1_w, L0_attn_mlp1_b, L0_attn_mlp2_w, L0_attn_mlp2_b,
           L0_ffn_Wq_pk, L0_ffn_pk_keys, L0_ffn_Wq, L0_ffn_keys_table, L0_ffn_values_table, L0_ffn_Wo):
    import concourse.bacc as bacc
    from concourse.bass_utils import run_bass_kernel_spmd as run

    a = {k: np.asarray(v) for k, v in locals().items() if k not in ("bacc", "run")}
    f = {k: v.astype(np.float32) for k, v in shape_constants().items()}
    col = lambda v: v.reshape(-1, 1)
    w_tok = np.zeros((4, 4, GRID, GRID, C), np.float32)
    for m, (row, column) in enumerate([(0, 0), (1, 0), (0, 1), (1, 1), (3, 2), (2, 3), (3, 3)]):
        for j in range(GRID):
            w_tok[row, column, j, j] = a["L0_tok_W"][m]
    qkv_w, qkv_b = a["L0_attn_qkv_w"], a["L0_attn_qkv_b"]
    rows = np.concatenate([a["L0_ffn_keys_table"], a["L0_ffn_values_table"]], axis=1)
    f.update({
        "x": a["x"],
        "w_tok": w_tok.reshape(128, -1),
        "tok_b": col(a["L0_tok_b"]), "cls_tok": col(a["cls_tok"]),
        "w_qk": qkv_w[0:2 * C].T, "b_qk": col(qkv_b[0:2 * C]),
        "w_v": qkv_w[2 * C:].T, "b_v": np.broadcast_to(qkv_b[2 * C:], (L, C)),
        "w_proj": a["L0_attn_proj_w"].T, "b_proj": col(a["L0_attn_proj_b"]),
        "q_scale": col(np.repeat(a["L0_attn_logit_scale"], HD)),
        "mlp1": np.concatenate([a["L0_attn_mlp1_w"].T, a["L0_attn_mlp1_b"][None]]),
        "mlp2": np.concatenate([a["L0_attn_mlp2_w"].T, a["L0_attn_mlp2_b"][None]]),
        "w_q2": a["L0_ffn_Wq"],
        "w_o2": a["L0_ffn_Wo"].reshape(H, C, C).transpose(1, 0, 2).reshape(C, H * C),
        "pk_q": a["L0_ffn_Wq_pk"].reshape(C, 2, H, DK).transpose(3, 2, 1, 0).reshape(DK, 2 * H, C),
        "pk_k": a["L0_ffn_pk_keys"].transpose(3, 2, 0, 1).reshape(DK, 2 * H, NK),
        "table": rows.reshape(H, CH, 128, 128).transpose(2, 0, 1, 3).reshape(128, H, CH * 128),
    })
    nc = bacc.Bacc("TRN2", target_bir_lowering=False, num_devices=1)
    arrays, dram = {}, {}
    for name, v in f.items():
        v = np.ascontiguousarray(v)
        arrays[f"in_{name}"] = v
        dram[name] = nc.dram_tensor(f"in_{name}", v.shape, mybir.dt.from_np(v.dtype), kind="ExternalInput").ap()
    dram["out"] = nc.dram_tensor("out", (B, L, C), F32, kind="ExternalOutput").ap()
    build(nc, dram)
    r = run(nc, [arrays], core_ids=[0])
    return r.results[0]["out"]
```

```python
from contextlib import ExitStack

import numpy as np

import concourse.bass as bass
from concourse import mybir

F32 = mybir.dt.float32
F32R = mybir.dt.float32r
ALU = mybir.AluOpType
ACT = mybir.ActivationFunctionType
AX = mybir.AxisListType

B, IMG, C = 64, 112, 64
GRID = 8
L = GRID * GRID + 1
H, HD = 8, 8
META = 96
NK, DK, TOPK = 64, 32, 16
NB = 8
T = NB * L
ITERS = B // NB
HALF = T // 2
TT, NT = T // 5, 5
CH = NK * NK // 128
UNITS = 2 * CH
SLOTS = UNITS // 2
RING = 6
R0 = 4
R1 = 3
NCAND = R0 * TOPK + (TOPK - R0) * R1
LOWEST = -3.0e38
MASKED = -1.0e30
EXP_CAP = 80.0
ROUNDING = 2.0 ** -20
EPS = 1e-5
SCALE2 = float(C) ** -0.5
ROWS = 24
MAPS, TOK, LN1, QK, VAL, NRM, ATT = ROWS + 2, ROWS + 4, ROWS + 6, ROWS + 17, ROWS + 21, ROWS + 23, ROWS + 32
TASKS, PERIOD = 2 * NB, 6
PROJ = ATT + TASKS * PERIOD + 11
LN2 = PROJ + 4


def shape_constants():
    def resize(n):
        scale = n / GRID
        x = (np.arange(GRID) + 0.5) * scale - 0.5
        w = np.maximum(0.0, 1.0 - np.abs(x[:, None] - np.arange(n)[None, :]) / scale)
        return w / w.sum(axis=1, keepdims=True)

    def haar(n):
        lo, hi = np.zeros((n // 2, n)), np.zeros((n // 2, n))
        i = np.arange(n // 2)
        lo[i, 2 * i] = lo[i, 2 * i + 1] = hi[i, 2 * i] = 0.7071067811865476
        hi[i, 2 * i + 1] = -0.7071067811865476
        return lo, hi

    lo1, hi1 = haar(IMG)
    lo2, hi2 = haar(IMG // 2)
    r1, r2 = resize(IMG // 2), resize(IMG // 4)
    filters = np.concatenate([r2 @ lo2 @ lo1, r2 @ hi2 @ lo1, r1 @ lo1, r1 @ hi1])
    d = np.arange(-(L - 1), L)
    rel = np.stack([0.0 * d, np.sign(d) * np.log1p(np.abs(d)), np.ones(len(d))])
    part = np.arange(128)
    spread = np.zeros((128, CH, 128))
    for c in range(CH):
        spread[part % NK, c, part] = 1.0
        spread[NK + 2 * c + part // NK, c, part] = 1.0
    causal = np.where(np.arange(L)[None, :] <= np.arange(L)[:, None], 0.0, MASKED)
    return {
        "filters": filters.T,
        "rel": rel,
        "spread": spread.reshape(128, CH * 128),
        "ident": np.eye(128),
        "head_of": np.kron(np.eye(2 * H), np.ones((HD, 1))),
        "center": np.eye(C) - 1.0 / C,
        "causal": causal,
    }


def build(nc, d):
    with ExitStack() as ctx:
        def sb(name, shape, dt=F32):
            return ctx.enter_context(nc.sbuf_tensor(name, shape, dt))

        pass_sems = []

        def bsem(name):
            s = ctx.enter_context(nc.semaphore(name))
            pass_sems.append(s)
            return s

        image_in = bsem("image_in")
        rows_mm, rows_out = bsem("rows_mm"), bsem("rows_out")
        maps_mm, maps_out = bsem("maps_mm"), bsem("maps_out")
        tok_mm, cls_set, h1_ready = bsem("tok_mm"), bsem("cls_set"), bsem("h1_ready")
        cen_mm, sq_ready, cen_out, var_mm = bsem("cen_mm"), bsem("sq_ready"), bsem("cen_out"), bsem("var_mm")
        std_ready, inv_ready, inv_mm, ln_ready = (
            bsem("std_ready"), bsem("inv_ready"), bsem("inv_mm"), bsem("ln_ready"))
        qk_mm, qk_out, qk_sq, v_mm, v_out = (
            bsem("qk_mm"), bsem("qk_out"), bsem("qk_sq"), bsem("v_mm"), bsem("v_out"))
        nrm_spread = bsem("nrm_spread")
        nrm_mm, nrm_ready, nrm_max, nrm_inv, nrm_turned, qk_unit = (
            bsem("nrm_mm"), bsem("nrm_ready"), bsem("nrm_max"), bsem("nrm_inv"), bsem("nrm_turned"), bsem("qk_unit"))
        kx_ready, s_mm, s_add, s_red, s_sub, s_exp, s_sum, s_inv = (
            bsem("kx_ready"), bsem("s_mm"), bsem("s_add"), bsem("s_red"), bsem("s_sub"), bsem("s_exp"),
            bsem("s_sum"), bsem("s_inv"))
        pt_mm, pt_out, o_mm, o_out, ot_mm, ot_out, proj_mm, h2_ready = (
            bsem("pt_mm"), bsem("pt_out"), bsem("o_mm"), bsem("o_out"), bsem("ot_mm"), bsem("ot_out"),
            bsem("proj_mm"), bsem("h2_ready"))
        front_sems = [s for s in pass_sems if s is not ln_ready]
        sc_mm, sc_out, shift_ready, z_ready, rz_ready, st_mm, hi_ready, st_ready = (
            bsem("sc_mm"), bsem("sc_out"), bsem("shift_ready"), bsem("z_ready"), bsem("rz_ready"),
            bsem("st_mm"), bsem("hi_ready"), bsem("st_ready"))
        pool_link, best_ready, cand_ready, top_ready, sc_shifted = (
            bsem("pool_link"), bsem("best_ready"), bsem("cand_ready"), bsem("top_ready"), bsem("sc_shifted"))
        a_ready, e_ready, w_ready, out_done, kv_ready = (
            bsem("a_ready"), bsem("e_ready"), bsem("w_ready"), bsem("out_done"), bsem("kv_ready"))
        q2_mm, q2_out, s2_mm, s2_add, s2_red, s2_sub, s2_exp, s2_sum, s2_inv, p2_ready = (
            bsem("q2_mm"), bsem("q2_out"), bsem("s2_mm"), bsem("s2_add"), bsem("s2_red"), bsem("s2_sub"),
            bsem("s2_exp"), bsem("s2_sum"), bsem("s2_inv"), bsem("p2_ready"))
        pt2_mm, pt2_out, v2_mm, v2_out, o2_mm, o2_out, ffn_mm, ffn_added = (
            bsem("pt2_mm"), bsem("pt2_out"), bsem("v2_mm"), bsem("v2_out"), bsem("o2_mm"), bsem("o2_out"),
            bsem("ffn_mm"), bsem("ffn_added"))
        attend_sems = pass_sems[pass_sems.index(s2_mm):]
        y_mm, y_out, y_stored = bsem("y_mm"), bsem("y_out"), bsem("y_stored")
        h_moved = bsem("h_moved")

        def sem(name):
            return ctx.enter_context(nc.semaphore(name))

        consts_in, spread_in = sem("consts_in"), sem("spread_in")
        tables_in = [sem(f"table{h}_in") for h in range(H)]
        set_mm, set_act, set_dve, set_pool = sem("set_mm"), sem("set_act"), sem("set_dve"), sem("set_pool")
        pass_end, pass_clear = sem("pass_end"), sem("pass_clear")

        table = sb("table", [128, H, CH, 128])
        spread = sb("spread", [128, CH * 128], F32R)
        spread_f = table[:, H - 1, :, :].rearrange("p c n -> p (c n)")
        ident = sb("ident", [128, 128])
        filters = sb("filters", [IMG, 32])
        w_tok = sb("w_tok", [128, GRID, C])
        tok_b, cls_tok, b_proj = sb("tok_b", [128, 1])[C:128, :], sb("cls_tok", [128, 1])[C:128, :], \
            sb("b_proj", [128, 1])[C:128, :]
        v_center = sb("v_center", [128, C])
        w_v, center = v_center[0:C, :], v_center[C:128, :]
        head_of = sb("head_of", [128, 2 * H])
        w_qk, b_qk = sb("w_qk", [C, 128]), sb("b_qk", [128, 1])
        b_v, w_proj = sb("b_v", [L, C]), sb("w_proj", [C, C])
        q_scale = sb("q_scale", [C, 1])
        mlp2 = sb("mlp2", [META + 1, H])
        pos_bias = sb("pos_bias", [L, H, L])
        causal = sb("causal", [L, L])
        pk_q, pk_k = (table[0:DK, H - 2, 0:8, :].rearrange("p c n -> p (c n)").rearrange("p (g n) -> p g n", g=16),
                      table[0:DK, H - 2, 8:16, :].rearrange("p c n -> p (c n)").rearrange("p (g n) -> p g n", g=16))
        w_sim = sb("w_sim", [C, H, 2 * NK])
        w_q2, w_o2 = sb("w_q2", [C, H * C]), sb("w_o2", [C, H, C])
        eps, mean = sb("eps", [128, 1]), sb("mean", [C, 1])

        h_sb, xh = sb("h_sb", [C, T]), sb("xh", [C, T])
        wts = sb("wts", [128, RING, HALF])
        kv = sb("kv", [128, T])
        rz_row = sb("rz_row", [128, 2, T])
        st_hi, st_lo = sb("st_hi", [128, 2, T], F32R), sb("st_lo", [128, 2, T], F32R)
        q2, s2, pt2 = sb("q2", [C, T]), sb("s2", [128, T]), sb("pt2", [L, T])
        o2, v2 = q2, s2[0:L, 0:NB * C].rearrange("p (b c) -> p b c", b=NB)
        y_sb = s2[0:TT, 0:NT * C]
        sc = sb("sc", [TT, 4, 2 * NK])
        best = sb("best", [TT, 2, 2, TOPK])
        rest = sb("rest", [TT, 2, NK])
        cand, cand_rest = sb("cand", [TT, NCAND]), sb("cand_rest", [TT, NCAND])
        top = sb("top", [TT, 4, 24])
        stat = sb("stat", [TT, 4, 4])
        cand_e = sb("cand_e", [TT, TOPK])
        red2 = sb("red2", [L, 2, NB])

        hx = sb("hx", [128, T])
        xf, hf = hx[0:C, :], hx[C:128, :]
        qk = sb("qk", [128, T])
        vf = sb("vf", [L, NB, C])
        scratch = sb("scratch", [128, 4, HALF])
        scratch_v = scratch[:, :, :].rearrange("p a t -> p (a t)")
        image = scratch_v[0:IMG, 0:NB * IMG].rearrange("p (b x) -> p b x", b=NB)
        sq = scratch_v[:, 0:T]
        inv = scratch_v[0:L, 0:NB * 128].rearrange("p (b c) -> p b c", b=NB)
        expo, pt = scratch[0:L, 0:2, :], scratch[0:L, 2:4, :]
        hid, rel, mlp1 = (wts[0:META + 1, 0, 0:2 * L - 1], wts[0:3, 1, 0:2 * L - 1],
                          wts[0:3, 2, 0:META])
        kx_t = sb("kx", [128, 2, HALF])
        kx = kx_t[0:C, :, :].rearrange("p a (h m) -> p a h m", h=H // 2)
        rows, maps = kx_t[0:IMG, 0, 0:NB * 32], kx_t[:, 1, 0:NB * GRID]
        nrm_t = sb("nrm", [L, 2 * C])
        nrm, o_tok = (nrm_t[:, :].rearrange("p (b h) -> p b h", b=NB),
                      nrm_t[:, :].rearrange("p (a c) -> p a c", a=2))
        std = sb("std", [L, NB])
        red = sb("red", [L, 2, 2, H // 2])
        ps = ctx.enter_context(nc.psum_tensor("ps", [128, 8, 512], F32))
        NA, FR, ACC, TK, AT = 3, 3, 4, 5, 6

        def bank(stage, kind):
            return {"scores": 0, "weights": FR, "output": 1, "turned": 2}[stage] if kind == "first" else FR

        def pair(parts):
            return ps[0:parts, AT:AT + 2, 0:HALF]

        def halves(ap):
            return ap.rearrange("p (s t) -> p s t", s=2)

        def half(ap, s):
            return ap[:, s * HALF:(s + 1) * HALF]

        x_v = d["x"].rearrange("b c y x -> y (b c) x")
        out_v = d["out"].rearrange("(i j) n c -> i (j n) c", j=NB).rearrange("i (t p) c -> i p t c", p=TT)

        consts = [(ident[:, :], "ident"), (filters[:, :], "filters"), (tok_b, "tok_b"), (cls_tok, "cls_tok"),
                  (center, "center"), (head_of[:, :], "head_of"), (w_qk[:, :], "w_qk"), (b_qk[:, :], "b_qk"),
                  (w_v, "w_v"), (b_v[:, :], "b_v"), (w_proj[:, :], "w_proj"), (b_proj, "b_proj"),
                  (q_scale[:, :], "q_scale"), (rel, "rel"), (mlp1, "mlp1"), (mlp2[:, :], "mlp2"),
                  (causal[:, :], "causal"), (w_q2[:, :], "w_q2"),
                  (w_tok[:, :, :].rearrange("p j c -> p (j c)"), "w_tok"),
                  (w_o2[:, :, :].rearrange("p h c -> p (h c)"), "w_o2"), (pk_q, "pk_q"), (pk_k, "pk_k")]

        def tile_at(u, step):
            t = (u - step) // 4
            return t if (u - step) % 4 == 0 and 0 <= t < NT else None

        def task_at(q, step):
            j = (q - ATT - step) // PERIOD
            return j if (q - ATT - step) % PERIOD == 0 and 0 <= j < TASKS else None

        def slots(kind):
            for hh in range(H + (kind == "last")):
                for u in range(SLOTS):
                    ahead = hh < H and (hh == H - 1 if kind == "first" else kind == "middle" or hh < H - 1)
                    yield (hh, u, hh * SLOTS + u, kind != "first" and hh < H, kind != "last", ahead,
                           kind != "first")

        def first_tile(kind, hh):
            return 0 if kind == "first" else NT * hh

        block = ctx.enter_context(nc.Block())

        @block.sync
        def _(sp):
            sp.dma_start(image, x_v[:, 0:NB, :]).then_inc(image_in, 16)
            for tile, name in consts:
                sp.dma_start(tile, d[name]).then_inc(consts_in, 16)
            sp.dma_start(spread_f, d["spread"]).then_inc(spread_in, 16)
            for h in range(H - 2):
                sp.dma_start(table[:, h, :, :].rearrange("p c n -> p (c n)"), d["table"][:, h, :])\
                  .then_inc(tables_in[h], 16)
            sp.wait_ge(consts_in, 16 * len(consts))
            sp.wait_ge(spread_in, 16)
            sp.wait_ge(set_mm, 2)
            sp.wait_ge(set_dve, 2)
            for h in range(H - 2, H):
                sp.dma_start(table[:, h, :, :].rearrange("p c n -> p (c n)"), d["table"][:, h, :])\
                  .then_inc(tables_in[h], 16)
            sp.drain().then_inc(pass_end, 1)
            sp.wait_ge(pass_clear, 1)
            with sp.Fori(0, ITERS - 1) as it:
                sp.dma_start(image, x_v[:, bass.ds(it * NB + NB, NB), :]).then_inc(image_in, 16)
                sp.wait_ge(y_out, 1)
                sp.dma_start(out_v[bass.ds(it, 1), :, :, :].rearrange("i p t c -> (i p) t c"),
                             y_sb.rearrange("p (t c) -> p t c", t=NT)).then_inc(y_stored, 16)
                sp.wait_ge(y_stored, 16)
                sp.drain().then_inc(pass_end, 1)
                sp.wait_ge(pass_clear, it + 2)
                sp.nop(nofuse=True)
            for k, block_id in enumerate([ITERS - 1, 0]):
                sp.wait_ge(y_out, k + 1)
                sp.dma_start(out_v[block_id, :, :, :], y_sb.rearrange("p (t c) -> p t c", t=NT))\
                    .then_inc(y_stored, 16)
                sp.wait_ge(y_stored, 16 * (k + 1))

        @block.gpsimd
        def _(pool):
            P = nc.gpsimd
            P.memset(eps[:, :], EPS).then_inc(set_pool, 1)
            P.memset(mean[:, :], 1.0 / C).then_inc(set_pool, 1)
            P.memset(kv[:, :], 0.0).then_inc(set_pool, 1)
            P.memset(q2[:, :], 0.0).then_inc(set_pool, 1)
            P.memset(h_sb[:, :], 0.0).then_inc(set_pool, 1)
            pool.wait_ge(set_pool, 5)
            pool.wait_ge(consts_in, 16 * len(consts))

            def front(q, kind):
                for s in range(2):
                    if q == NRM + 4 + s:
                        pool.wait_ge(nrm_inv, 1)
                        P.tensor_copy(inv[:, 4 * s:4 * s + 4, :].rearrange("p b (h d) -> p b h d", d=HD),
                                      nrm[:, 4 * s:4 * s + 4, :].unsqueeze(3).to_broadcast([L, 4, 2 * H, HD]))\
                            .then_inc(nrm_spread, 1)
                j = task_at(q, -2)
                if j is not None:
                    b, s = j // 2, j % 2
                    pool.wait_ge(qk_unit, 4)
                    if j >= 2:
                        pool.wait_ge(s_mm, j - 1)
                    P.tensor_tensor(kx[:, j % 2, :, :],
                                    xf[:, b * L:(b + 1) * L].unsqueeze(1).to_broadcast([C, H // 2, L]),
                                    head_of[0:C, 4 * s:4 * s + 4].unsqueeze(2)
                                    .to_broadcast([C, H // 2, L]), ALU.mult).then_inc(kx_ready, 1)
                j = task_at(q, 3)
                if j is not None:
                    pool.wait_ge(s_red, j + 1)
                    e = expo[:, j % 2, :].rearrange("p (h m) -> p h m", h=H // 2)
                    P.tensor_tensor(e, e, red[:, j % 2, 0, :].unsqueeze(2).to_broadcast([L, H // 2, L]),
                                    ALU.subtract).then_inc(s_sub, 1)

            def candidates(n):
                pool.wait_ge(best_ready, 6 * (n + 1))
                if n >= 1:
                    pool.wait_ge(top_ready, 5 * (n - 1) + 2)
                b0, b1 = best[:, n % 2, 0, :], best[:, n % 2, 1, :]
                P.tensor_tensor(cand[:, 0:R0 * TOPK].rearrange("p (a b) -> p a b", a=R0),
                                b0[:, 0:R0].unsqueeze(2).to_broadcast([TT, R0, TOPK]),
                                b1.unsqueeze(1).to_broadcast([TT, R0, TOPK]), ALU.add)
                P.tensor_tensor(cand[:, R0 * TOPK:NCAND].rearrange("p (a b) -> p a b", b=R1),
                                b0[:, R0:TOPK].unsqueeze(2).to_broadcast([TT, TOPK - R0, R1]),
                                b1[:, 0:R1].unsqueeze(1).to_broadcast([TT, TOPK - R0, R1]), ALU.add)\
                    .then_inc(cand_ready, 1)

            def threshold(n):
                tp, st = top[:, n % 4, :], stat[:, n % 4, :]
                pool.wait_ge(top_ready, 5 * (n + 1))
                P.tensor_scalar(st[:, 1:2], tp[:, 15:16], tp[:, 16:17], -0.5, ALU.add, ALU.mult)
                P.tensor_scalar(st[:, 0:1], st[:, 0:1], ROUNDING, tp[:, 15:16], ALU.mult, ALU.subtract)\
                    .then_inc(pool_link, 1)
                pool.wait_ge(pool_link, 2 * n + 1)
                P.tensor_scalar(st[:, 0:1], st[:, 0:1], st[:, 1:2], tp[:, 0:1], ALU.min, ALU.add)\
                    .then_inc(pool_link, 1)
                pool.wait_ge(pool_link, 2 * n + 2)
                P.tensor_scalar(st[:, 1:2], st[:, 0:1], EXP_CAP, tp[:, 0:1], ALU.min, ALU.subtract)\
                    .then_inc(shift_ready, 1)
                pool.wait_ge(shift_ready, n + 1)
                P.tensor_scalar(sc[:, n % 4, 0:NK], sc[:, n % 4, 0:NK], st[:, 1:2], None, ALU.add)\
                    .then_inc(sc_shifted, 1)

            def attend(hh, u):
                s = s2[0:L, :].rearrange("p (b m) -> p b m", b=NB)
                if u == 5:
                    pool.wait_ge(s2_red, hh + 1)
                    P.tensor_tensor(s, s, red2[:, 0, :].unsqueeze(2).to_broadcast([L, NB, L]), ALU.subtract)\
                        .then_inc(s2_sub, 1)
                if u == 10:
                    pool.wait_ge(s2_inv, hh + 1)
                    P.tensor_tensor(s, s, red2[:, 1, :].unsqueeze(2).to_broadcast([L, NB, L]), ALU.mult)\
                        .then_inc(p2_ready, 1)

            def run(kind):
                for hh, u, q, dense, front_on, ahead, behind in slots(kind):
                    n0 = first_tile(kind, hh)
                    if ahead and tile_at(u, 4) is not None:
                        candidates(n0 + tile_at(u, 4))
                    if ahead and tile_at(u, 10) is not None:
                        threshold(n0 + tile_at(u, 10))
                    if behind:
                        attend(hh, u)
                    if front_on:
                        front(q, kind)
                    if kind != "last" and hh == H - 1 and u == 0:
                        pool.wait_ge(ln_ready, 4)
                        for s in front_sems:
                            pool.sem_clear(s)
                    if kind == "middle" and hh == H - 1 and u == 30:
                        pool.wait_ge(q2_out, H)
                        for s in attend_sems:
                            pool.sem_clear(s)

            def clear():
                early = front_sems + attend_sems
                for s in pass_sems:
                    if s not in early:
                        pool.sem_clear(s)
                pool.nop().then_inc(pass_clear, 1)

            run("first")
            pool.wait_ge(pass_end, 4)
            pool.nop(nofuse=True)
            clear()
            with pool.Fori(0, ITERS - 1) as it:
                run("middle")
                pool.wait_ge(pass_end, it * 4 + 8)
                pool.nop(nofuse=True)
                clear()
            run("last")

        @block.tensor
        def _(pe):
            mm = nc.tensor.matmul
            tr = nc.tensor.transpose
            pe.wait_ge(consts_in, 16 * len(consts))
            mm(ps[0:META, 0, 0:2 * L - 1], mlp1, rel, start=True, stop=True).then_inc(set_mm, 1)
            for g in range(2 * H):
                last = mm(ps[0:C, 2 + g // 8, (g % 8) * NK:(g % 8 + 1) * NK], pk_q[:, g, :], pk_k[:, g, :],
                          start=True, stop=True)
            last.then_inc(set_mm, 1)
            pe.wait_ge(set_act, 1)
            pe.wait_ge(set_dve, 1)
            for m in range(L):
                last = mm(ps[0:L, 4 + m // NK, (m % NK) * H:(m % NK + 1) * H], hid[:, L - 1 - m:2 * L - 1 - m],
                          mlp2[:, :], start=True, stop=True)
            last.then_inc(set_mm, 1)
            pe.wait_ge(set_act, 4)
            pe.wait_ge(set_pool, 5)

            def layernorm(q, n, start):
                for s in range(2):
                    if q == start + 2 * s:
                        if s == 1:
                            pe.wait_ge(cen_out, 2 * n + 1)
                        elif n == 0:
                            pe.wait_ge(h1_ready, 1)
                            pe.wait_ge(cls_set, 1)
                        else:
                            pe.wait_ge(h2_ready, 2)
                        mm(ps[0:C, FR, 0:HALF], center, half(hf, s), start=True, stop=True).then_inc(cen_mm, 1)
                    if q == start + 7 + 2 * s:
                        if s == 0:
                            pe.wait_ge(inv_ready, n + 1)
                        else:
                            pe.wait_ge(ln_ready, 2 * n + 1)
                        for b in range(4):
                            last = tr(ps[0:C, FR, b * L:(b + 1) * L],
                                      std[:, 4 * s + b:4 * s + b + 1].to_broadcast([L, C]), ident[0:L, 0:L])
                        last.then_inc(inv_mm, 1)
                if q == start + 4:
                    pe.wait_ge(sq_ready, 2 * n + 2)
                    pe.wait_ge(cen_out, 2 * n + 2)
                    for b in range(NB):
                        last = mm(ps[0:L, FR, b:b + 1], sq[0:C, b * L:(b + 1) * L], mean[:, :],
                                  start=True, stop=True)
                    last.then_inc(var_mm, 1)

            def front(q, kind):
                alone = kind == "first"
                if q == ROWS:
                    pe.wait_ge(image_in, 16)
                    for b in range(NB):
                        last = mm(ps[0:IMG, FR, b * 32:(b + 1) * 32], image[:, b, :], filters[:, :],
                                  start=True, stop=True)
                    last.then_inc(rows_mm, 1)
                if q == MAPS:
                    pe.wait_ge(rows_out, 1)
                    rows_v = rows.rearrange("p (b r i) -> p b r i", b=NB, r=4)
                    for r in range(4):
                        last = mm(ps[32 * r:32 * r + 32, FR, 0:NB * GRID], filters[:, :], rows_v[:, :, r, :],
                                  start=True, stop=True)
                    last.then_inc(maps_mm, 1)
                if q == TOK:
                    pe.wait_ge(maps_out, 1)
                    for j in range(GRID):
                        last = mm(ps[C:128, FR, j * 64:(j + 1) * 64], w_tok[:, j, :], maps, start=True, stop=True)
                    last.then_inc(tok_mm, 1)
                layernorm(q, 0, LN1)
                for s in range(2):
                    if q == QK + 2 * s:
                        pe.wait_ge(ln_ready, 2)
                        if s == 1:
                            pe.wait_ge(qk_out, 1)
                        mm(ps[0:128, FR, 0:HALF], w_qk[:, :], half(xf, s), start=True, stop=True).then_inc(qk_mm, 1)
                if q == VAL:
                    pe.wait_ge(qk_out, 2)
                    for b in range(NB):
                        last = mm(ps[0:L, FR, b * C:(b + 1) * C], xf[:, b * L:(b + 1) * L], w_v,
                                  start=True, stop=True)
                    last.then_inc(v_mm, 1)
                if q == NRM:
                    pe.wait_ge(v_out, 1)
                    pe.wait_ge(qk_sq, 2)
                    for b in range(NB):
                        last = mm(ps[0:L, FR, b * 2 * H:(b + 1) * 2 * H], sq[:, b * L:(b + 1) * L], head_of[:, :],
                                  start=True, stop=True)
                    last.then_inc(nrm_mm, 1)
                for s in range(2):
                    if q == NRM + 5 + 2 * s:
                        pe.wait_ge(nrm_spread, s + 1)
                        if s == 1:
                            pe.wait_ge(qk_unit, 2)
                        for b in range(4):
                            last = tr(ps[0:128, FR, b * L:(b + 1) * L], inv[:, 4 * s + b, :], ident[0:L, 0:L])
                        last.then_inc(nrm_turned, 1)
                j = task_at(q, 0)
                if j is not None:
                    b = j // 2
                    pe.wait_ge(kx_ready, j + 1)
                    if j >= 1 and (alone or j == 1):
                        pe.wait_ge(s_add, j)
                    if j >= 2 and not alone:
                        pe.wait_ge(o_out, j - 1)
                    mm(ps[0:L, bank("scores", kind), 0:HALF], qk[0:C, b * L:(b + 1) * L], kx[:, j % 2, :, :]
                       .rearrange("p h m -> p (h m)"), start=True, stop=True).then_inc(s_mm, 1)
                j = task_at(q, 8)
                if j is not None:
                    pe.wait_ge(s_exp, j + 1)
                    if j >= 1 and alone:
                        pe.wait_ge(pt_out, j)
                    elif not alone and j < TASKS - 1:
                        pe.wait_ge(s_add, j + 2)
                    elif not alone:
                        pe.wait_ge(o_out, TASKS - 1)
                    for h in range(4):
                        last = tr(ps[0:L, bank("weights", kind), h * L:(h + 1) * L],
                                  expo[:, j % 2, h * L:(h + 1) * L], ident[0:L, 0:L])
                    last.then_inc(pt_mm, 1)
                j = task_at(q, 15)
                if j is not None and j % 2 == 1:
                    pe.wait_ge(o_out, j + 1)
                    if j >= 3 and alone:
                        pe.wait_ge(ot_out, j // 2)
                    if not alone:
                        pe.wait_ge(pt_out, min(j + 2, TASKS))
                    tr(ps[0:C, bank("turned", kind), 0:L], o_tok[:, (j // 2) % 2, :], ident[0:L, 0:L])\
                        .then_inc(ot_mm, 1)
                j = task_at(q, 10)
                if j is not None:
                    b, s = j // 2, j % 2
                    pe.wait_ge(pt_out, j + 1)
                    if j >= 1 and alone:
                        pe.wait_ge(o_out, j)
                    if j >= 2 and not alone:
                        pe.wait_ge(ot_out, j // 2 if s == 0 else (j - 1) // 2)
                    for h in range(4):
                        last = mm(ps[0:L, bank("output", kind), h * HD:(h + 1) * HD],
                                  pt[:, j % 2, h * L:(h + 1) * L],
                                  vf[:, b, (4 * s + h) * HD:(4 * s + h + 1) * HD], start=True, stop=True)
                    last.then_inc(o_mm, 1)
                for s in range(2):
                    if q == PROJ + 2 * s:
                        pe.wait_ge(ot_out, NB)
                        if s == 1:
                            pe.wait_ge(h2_ready, 1)
                        mm(ps[C:128, FR, 0:HALF], w_proj[:, :], half(xf, s), start=True, stop=True)\
                            .then_inc(proj_mm, 1)
                layernorm(q, 1, LN2)

            def scores(n, h, t):
                if n >= 1:
                    pe.wait_ge(sc_out, n)
                if n % NT >= 4 or n >= NT:
                    pe.wait_ge(st_ready, n - n % NT + max(0, n % NT - 3))
                if h == H:
                    pe.wait_ge(ln_ready, 4)
                src = xf if h == H else xh
                mm(ps[0:TT, TK, 0:128], src[:, t * TT:(t + 1) * TT], w_sim[:, h % H, :],
                   start=True, stop=True).then_inc(sc_mm, 1)

            def turn_scores(n):
                pe.wait_ge(sc_shifted, n + 1)
                pe.wait_ge(rz_ready, n + 1)
                pe.wait_ge(sc_out, n - n % NT + min(n % NT + 4, NT))
                if n >= 1:
                    pe.wait_ge(st_ready, n)
                tr(ps[0:128, TK, 128:128 + TT], sc[:, n % 4, :], ident[0:TT, 0:TT])
                tr(ps[0:128, TK, 256:256 + TT], stat[:, n % 4, 3:4].to_broadcast([TT, 128]), ident[0:TT, 0:TT])\
                    .then_inc(st_mm, 1)

            def spread_scores(g):
                if g >= H * UNITS:
                    return
                h, w = g // UNITS, g % UNITS
                s, c = w // CH, w % CH
                if w == 0 and h > 0:
                    pe.wait_ge(st_ready, NT * h)
                if g >= NA:
                    pe.wait_ge(w_ready, g - NA + 1)
                k = spread[:, c * 128:(c + 1) * 128]
                o = ps[0:128, g % NA, 0:HALF]
                mm(o, k, half(st_hi[:, h % 2, :], s), start=True, stop=False)
                mm(o, k, half(st_lo[:, h % 2, :], s), start=False, stop=True).then_inc(a_ready, 1)

            def add_rows(g):
                h, c = g // UNITS, g % CH
                pe.wait_ge(w_ready, g + 1)
                if g % UNITS == 0:
                    pe.wait_ge(tables_in[h], 16)
                if c == 0 and g > 0:
                    pe.wait_ge(kv_ready, g // CH)
                mm(ps[0:128, ACC, 0:HALF], table[:, h, c, :], wts[:, g % RING, :],
                   start=(c == 0), stop=(c == CH - 1)).then_inc(out_done, 1)

            def attend(hh, u):
                if u == 2:
                    if hh > 0:
                        pe.wait_ge(q2_out, hh)
                        pe.wait_ge(kv_ready, 2 * hh)
                    for b in range(NB):
                        last = mm(ps[0:L, AT + b // 4, (b % 4) * L:(b % 4 + 1) * L], q2[:, b * L:(b + 1) * L],
                                  kv[0:C, b * L:(b + 1) * L], start=True, stop=True)
                    last.then_inc(s2_mm, 1)
                if u == 12:
                    pe.wait_ge(p2_ready, hh + 1)
                    for b in range(NB):
                        last = tr(ps[0:L, AT + b // 4, (b % 4) * L:(b % 4 + 1) * L],
                                  s2[0:L, b * L:(b + 1) * L], ident[0:L, 0:L])
                    last.then_inc(pt2_mm, 1)
                if u == 14:
                    pe.wait_ge(pt2_out, hh + 1)
                    for b in range(NB):
                        last = tr(ps[0:L, AT, b * C:(b + 1) * C], kv[C:128, b * L:(b + 1) * L],
                                  ident[C:128, C:128])
                    last.then_inc(v2_mm, 1)
                if u == 16:
                    pe.wait_ge(v2_out, hh + 1)
                    for b in range(NB):
                        last = mm(ps[0:C, AT + b // 4, (b % 4) * L:(b % 4 + 1) * L], v2[:, b, :],
                                  pt2[:, b * L:(b + 1) * L], start=True, stop=True)
                    last.then_inc(o2_mm, 1)
                if u == 18:
                    pe.wait_ge(o2_out, hh + 1)
                    for s in range(2):
                        last = mm(ps[0:C, AT + s, 0:HALF], w_o2[:, (hh - 1) % H, :], half(o2, s),
                                  start=True, stop=True)
                    last.then_inc(ffn_mm, 1)
                if u == 20 and hh % H == 0:
                    pe.wait_ge(ffn_added, hh + 1)
                    for t in range(NT):
                        last = tr(ps[0:TT, AT, t * C:(t + 1) * C], h_sb[:, t * TT:(t + 1) * TT], ident[0:C, 0:C])
                    last.then_inc(y_mm, 1)
                if u == 28 and hh < H:
                    pe.wait_ge(ffn_added, hh + 1)
                    pe.wait_ge(y_out, 1)
                    for s in range(2):
                        last = mm(ps[0:C, AT + s, 0:HALF], w_q2[:, hh * C:(hh + 1) * C], half(xh, s),
                                  start=True, stop=True)
                    last.then_inc(q2_mm, 1)

            def run(kind):
                if kind != "first":
                    spread_scores(0)
                    spread_scores(1)
                for hh, u, q, dense, front_on, ahead, behind in slots(kind):
                    n0 = first_tile(kind, hh)
                    if dense:
                        spread_scores(2 * q + 2)
                        if q > 0:
                            add_rows(2 * q - 1)
                    if ahead and tile_at(u, 0) is not None:
                        scores(n0 + tile_at(u, 0), hh + 1, tile_at(u, 0))
                    if ahead and tile_at(u, 13) is not None:
                        turn_scores(n0 + tile_at(u, 13))
                    if behind:
                        attend(hh, u)
                    if front_on:
                        front(q, kind)
                    if dense:
                        spread_scores(2 * q + 3)
                        add_rows(2 * q)
                    if dense and q == H * SLOTS - 1:
                        add_rows(2 * q + 1)

            run("first")
            pe.drain().then_inc(pass_end, 1)
            pe.wait_ge(pass_clear, 1)
            with pe.Fori(0, ITERS - 1) as it:
                run("middle")
                pe.drain().then_inc(pass_end, 1)
                pe.wait_ge(pass_clear, it + 2)
            run("last")

        @block.scalar
        def _(act):
            A = nc.scalar.activation
            act.wait_ge(set_mm, 1)
            A(hid[0:META, :], ps[0:META, 0, 0:2 * L - 1], ACT.Relu).then_inc(set_act, 1)
            act.wait_ge(set_mm, 2)
            A(w_sim[:, :, :].rearrange("p h n -> p (h n)"),
              ps[0:C, 2:4, :].rearrange("p a n -> p (a n)"), ACT.Copy).then_inc(set_act, 1)
            act.wait_ge(set_mm, 3)
            A(pos_bias[:, :, 0:NK], ps[0:L, 4, :].rearrange("p (m h) -> p h m", h=H), ACT.Copy)\
                .then_inc(set_act, 1)
            A(pos_bias[:, :, NK:L], ps[0:L, 5, 0:H].rearrange("p (m h) -> p h m", h=H), ACT.Copy)\
                .then_inc(set_act, 1)
            act.wait_ge(set_dve, 3)
            A(q_scale[:, :], q_scale[:, :], ACT.Exp).then_inc(set_act, 1)
            act.wait_ge(set_pool, 1)

            def layernorm(q, n, start):
                for s in range(2):
                    if q == start + 2 * s:
                        act.wait_ge(cen_mm, 2 * n + s + 1)
                        A(half(sq[0:C, :], s), ps[0:C, FR, 0:HALF], ACT.Square).then_inc(sq_ready, 1)
                if q == start + 4:
                    act.wait_ge(var_mm, n + 1)
                    A(std[:, :], ps[0:L, FR, 0:NB], ACT.Sqrt, bias=eps[0:L, 0:1]).then_inc(std_ready, 1)

            def front(q, kind):
                if q == ROWS:
                    act.wait_ge(rows_mm, 1)
                    A(rows, ps[0:IMG, FR, 0:NB * 32], ACT.Copy).then_inc(rows_out, 1)
                if q == MAPS:
                    act.wait_ge(maps_mm, 1)
                    A(maps, ps[0:128, FR, 0:NB * GRID], ACT.Copy).then_inc(maps_out, 1)
                if q == TOK:
                    act.wait_ge(tok_mm, 1)
                    act.wait_ge(cls_set, 1)
                if TOK <= q < TOK + 2:
                    h_tok = hf.rearrange("p (b n) -> p b n", b=NB)[:, :, 1:L]\
                        .rearrange("p b (i j) -> p j b i", j=GRID)
                    tok = ps[C:128, FR, :].rearrange("p (j b i) -> p j b i", j=GRID, b=NB)
                    for j in range(4 * (q - TOK), 4 * (q - TOK) + 4):
                        last = A(h_tok[:, j, :, :], tok[:, j, :, :], ACT.Identity, bias=tok_b)
                    if q == TOK + 1:
                        last.then_inc(h1_ready, 1)
                layernorm(q, 0, LN1)
                for s in range(2):
                    if q == QK + 2 * s:
                        act.wait_ge(qk_mm, s + 1)
                        A(half(qk[:, :], s), ps[0:128, FR, 0:HALF], ACT.Identity, bias=b_qk[:, 0:1])\
                            .then_inc(qk_out, 1)
                    if q == QK + 2 * s + 1:
                        act.wait_ge(qk_out, s + 1)
                        A(half(sq, s), half(qk[:, :], s), ACT.Square).then_inc(qk_sq, 1)
                if q == NRM:
                    act.wait_ge(nrm_mm, 1)
                    A(nrm.rearrange("p b h -> p (b h)"), ps[0:L, FR, 0:2 * C], ACT.Sqrt).then_inc(nrm_ready, 1)
                j = task_at(q, 5)
                if j is not None:
                    act.wait_ge(s_sub, j + 1)
                    A(expo[:, j % 2, :], expo[:, j % 2, :], ACT.Exp).then_inc(s_exp, 1)
                j = task_at(q, 8)
                if j is not None:
                    act.wait_ge(pt_mm, j + 1)
                    if j >= 2:
                        act.wait_ge(o_mm, j - 1)
                    A(pt[:, j % 2, :], ps[0:L, bank("weights", kind), 0:HALF], ACT.Copy).then_inc(pt_out, 1)
                j = task_at(q, 15)
                if j is not None and j % 2 == 1:
                    act.wait_ge(ot_mm, j // 2 + 1)
                    A(xf[:, (j // 2) * L:(j // 2 + 1) * L], ps[0:C, bank("turned", kind), 0:L], ACT.Copy).then_inc(ot_out, 1)
                layernorm(q, 1, LN2)

            def scores(n):
                act.wait_ge(sc_mm, n + 1)
                if n >= 4:
                    act.wait_ge(st_mm, n - 3)
                A(sc[:, n % 4, :], ps[0:TT, TK, 0:128], ACT.Copy).then_inc(sc_out, 1)

            def partition_sum(n):
                act.wait_ge(shift_ready, n + 1)
                A(cand_e[:, :], top[:, n % 4, 0:TOPK], ACT.Exp, bias=stat[:, n % 4, 1:2],
                  accum_out=stat[:, n % 4, 2:3]).then_inc(z_ready, 1)

            def turned_scores(n, h, t):
                act.wait_ge(st_mm, n + 1)
                if h >= 2 and t == 0:
                    act.wait_ge(kv_ready, 2 * h - 2)
                A(rz_row[:, h % 2, t * TT:(t + 1) * TT], ps[0:128, TK, 256:256 + TT], ACT.Copy)
                A(st_hi[:, h % 2, t * TT:(t + 1) * TT], ps[0:128, TK, 128:128 + TT], ACT.Copy)\
                    .then_inc(hi_ready, 1)

            def exp_unit(g):
                act.wait_ge(a_ready, g + 1)
                if g >= RING:
                    act.wait_ge(out_done, g - RING + 1)
                A(wts[:, g % RING, :], ps[0:128, g % NA, 0:HALF], ACT.Exp).then_inc(e_ready, 1)

            def attend(hh, u):
                if u == 7:
                    act.wait_ge(s2_sub, hh + 1)
                    A(s2[0:L, :], s2[0:L, :], ACT.Exp).then_inc(s2_exp, 1)
                if u == 12:
                    act.wait_ge(pt2_mm, hh + 1)
                    A(halves(pt2[:, :]), pair(L), ACT.Copy).then_inc(pt2_out, 1)
                if u == 14:
                    act.wait_ge(v2_mm, hh + 1)
                    A(v2.rearrange("p b c -> p (b c)"), ps[0:L, AT, :], ACT.Copy).then_inc(v2_out, 1)
                if u == 16:
                    act.wait_ge(o2_mm, hh + 1)
                    A(halves(o2[:, :]), pair(C), ACT.Copy).then_inc(o2_out, 1)
                if u == 20 and hh % H == 0:
                    act.wait_ge(y_mm, hh // H + 1)
                    A(y_sb, ps[0:TT, AT, 0:NT * C], ACT.Copy).then_inc(y_out, 1)
                if u == 28 and hh < H:
                    act.wait_ge(q2_mm, hh + 1)
                    A(halves(q2[:, :]), pair(C), ACT.Copy, scale=SCALE2).then_inc(q2_out, 1)

            def run(kind):
                for hh, u, q, dense, front_on, ahead, behind in slots(kind):
                    n0 = first_tile(kind, hh)
                    if dense:
                        exp_unit(2 * q)
                        exp_unit(2 * q + 1)
                    if ahead and tile_at(u, 0) is not None:
                        scores(n0 + tile_at(u, 0))
                    if ahead and tile_at(u, 11) is not None:
                        partition_sum(n0 + tile_at(u, 11))
                    if ahead and tile_at(u, 13) is not None:
                        turned_scores(n0 + tile_at(u, 13), 0 if kind == "first" else hh + 1, tile_at(u, 13))
                    if behind:
                        attend(hh, u)
                    if front_on:
                        front(q, kind)

            run("first")
            act.drain().then_inc(pass_end, 1)
            act.wait_ge(pass_clear, 1)
            with act.Fori(0, ITERS - 1) as it:
                run("middle")
                act.drain().then_inc(pass_end, 1)
                act.wait_ge(pass_clear, it + 2)
            run("last")

        @block.vector
        def _(dve):
            V = nc.vector
            dve.wait_ge(consts_in, 16 * len(consts))
            V.memset(hid[META:META + 1, :], 1.0).then_inc(set_dve, 1)
            dve.wait_ge(spread_in, 16)
            V.tensor_copy(spread[:, :], spread_f).then_inc(set_dve, 1)
            V.tensor_scalar(q_scale[:, :], q_scale[:, :], float(np.log(1.0 / 0.01)), None, ALU.min)\
                .then_inc(set_dve, 1)
            dve.wait_ge(set_act, 5)

            def layernorm(q, n, start):
                for s in range(2):
                    if q == start + 2 * s + 1:
                        dve.wait_ge(sq_ready, 2 * n + s + 1)
                        V.tensor_copy(half(xf, s), ps[0:C, FR, 0:HALF]).then_inc(cen_out, 1)
                    if q == start + 8 + 2 * s:
                        dve.wait_ge(inv_mm, 2 * n + s + 1)
                        V.tensor_tensor(half(xf, s), ps[0:C, FR, 0:HALF], half(xf, s), ALU.mult)\
                            .then_inc(ln_ready, 1)
                if q == start + 6:
                    dve.wait_ge(std_ready, n + 1)
                    V.reciprocal(std[:, :], std[:, :]).then_inc(inv_ready, 1)

            def front(q, kind):
                if q == ROWS:
                    V.tensor_copy(hf.rearrange("p (b n) -> p b n", b=NB)[:, :, 0:1],
                                  cls_tok.unsqueeze(1).to_broadcast([C, NB, 1])).then_inc(cls_set, 1)
                layernorm(q, 0, LN1)
                if q == VAL + 1:
                    dve.wait_ge(v_mm, 1)
                    V.tensor_tensor(vf[:, :, :], ps[0:L, FR, :].rearrange("p (b c) -> p b c", b=NB),
                                    b_v[:, :].unsqueeze(1).to_broadcast([L, NB, C]), ALU.add).then_inc(v_out, 1)
                if q == NRM + 2:
                    dve.wait_ge(nrm_ready, 1)
                    V.tensor_scalar(nrm_t[:, :], nrm_t[:, :], 1e-12, None, ALU.max).then_inc(nrm_max, 1)
                if q == NRM + 3:
                    dve.wait_ge(nrm_max, 1)
                    V.reciprocal(nrm_t[:, :], nrm_t[:, :]).then_inc(nrm_inv, 1)
                for s in range(2):
                    if q == NRM + 6 + 2 * s:
                        dve.wait_ge(nrm_turned, s + 1)
                        V.scalar_tensor_tensor(out=half(qk[0:C, :], s), in0=ps[0:C, FR, 0:HALF],
                                               scalar=q_scale[:, 0:1], in1=half(qk[0:C, :], s),
                                               op0=ALU.mult, op1=ALU.mult).then_inc(qk_unit, 1)
                        V.tensor_tensor(half(xf, s), ps[C:128, FR, 0:HALF], half(qk[C:128, :], s), ALU.mult)\
                            .then_inc(qk_unit, 1)
                j = task_at(q, 1)
                if j is not None:
                    dve.wait_ge(s_mm, j + 1)
                    if j >= 2:
                        dve.wait_ge(pt_mm, j - 1)
                    V.tensor_tensor(expo[:, j % 2, :], ps[0:L, bank("scores", kind), 0:HALF],
                                    pos_bias[:, 4 * (j % 2):4 * (j % 2) + 4, :].rearrange("p h m -> p (h m)"),
                                    ALU.add).then_inc(s_add, 1)
                j = task_at(q, 2)
                if j is not None:
                    dve.wait_ge(s_add, j + 1)
                    V.tensor_reduce(red[:, j % 2, 0, :], expo[:, j % 2, :].rearrange("p (h m) -> p h m", h=4),
                                    AX.X, ALU.max).then_inc(s_red, 1)
                j = task_at(q, 6)
                if j is not None:
                    dve.wait_ge(s_exp, j + 1)
                    V.tensor_reduce(red[:, j % 2, 1, :], expo[:, j % 2, :].rearrange("p (h m) -> p h m", h=4),
                                    AX.X, ALU.add).then_inc(s_sum, 1)
                j = task_at(q, 7)
                if j is not None:
                    dve.wait_ge(s_sum, j + 1)
                    V.reciprocal(red[:, j % 2, 1, :], red[:, j % 2, 1, :]).then_inc(s_inv, 1)
                j = task_at(q, 11)
                if j is not None:
                    b, s = j // 2, j % 2
                    dve.wait_ge(o_mm, j + 1)
                    dve.wait_ge(s_inv, j + 1)
                    if b >= 2:
                        dve.wait_ge(ot_mm, b - 1)
                    V.tensor_tensor(o_tok[:, b % 2, s * 32:s * 32 + 32].rearrange("p (h d) -> p h d", h=4),
                                    ps[0:L, bank("output", kind), 0:32].rearrange("p (h d) -> p h d", h=4),
                                    red[:, j % 2, 1, :].unsqueeze(2).to_broadcast([L, 4, HD]), ALU.mult)\
                        .then_inc(o_out, 1)
                for s in range(2):
                    if q == PROJ + 2 * s + 1:
                        dve.wait_ge(proj_mm, s + 1)
                        V.scalar_tensor_tensor(out=half(hf, s), in0=ps[C:128, FR, 0:HALF], scalar=b_proj,
                                               in1=half(hf, s), op0=ALU.add, op1=ALU.add).then_inc(h2_ready, 1)
                layernorm(q, 1, LN2)

            def best16(n, step):
                if step == 1:
                    dve.wait_ge(sc_out, n + 1)
                    if n >= 2:
                        dve.wait_ge(cand_ready, n - 1)
                else:
                    dve.wait_ge(best_ready, 6 * n + 2 * (step - 1))
                for side in range(2):
                    s = sc[:, n % 4, side * NK:(side + 1) * NK]
                    top8 = best[:, n % 2, side, 0:8]
                    if step == 1:
                        V.max(top8, s).then_inc(best_ready, 1)
                    if step == 2:
                        V.match_replace(rest[:, side, :], top8, s, LOWEST).then_inc(best_ready, 1)
                    if step == 3:
                        V.max(best[:, n % 2, side, 8:16], rest[:, side, :]).then_inc(best_ready, 1)

            def top24(n, step):
                if step == 0:
                    dve.wait_ge(cand_ready, n + 1)
                    if n >= 4:
                        dve.wait_ge(st_mm, n - 3)
                    V.tensor_reduce(stat[:, n % 4, 0:1], best[:, n % 2, :, :].rearrange("p s k -> p (s k)"),
                                    AX.X, ALU.max, apply_absolute_value=True)
                else:
                    dve.wait_ge(top_ready, 5 * n + step)
                k = step // 2
                src = cand[:, :] if step < 2 else cand_rest[:, :]
                if step % 2 == 0:
                    V.max(top[:, n % 4, 8 * k:8 * k + 8], src).then_inc(top_ready, 1)
                else:
                    V.match_replace(cand_rest[:, :], top[:, n % 4, 8 * k:8 * k + 8], src, LOWEST)\
                        .then_inc(top_ready, 1)

            def invert_sum(n):
                dve.wait_ge(z_ready, n + 1)
                V.reciprocal(stat[:, n % 4, 3:4], stat[:, n % 4, 2:3]).then_inc(rz_ready, 1)

            def low_part(n, h, t):
                dve.wait_ge(hi_ready, n + 1)
                V.tensor_tensor(st_lo[:, h % 2, t * TT:(t + 1) * TT], ps[0:128, TK, 128:128 + TT],
                                st_hi[:, h % 2, t * TT:(t + 1) * TT].bitcast(F32), ALU.subtract)\
                    .then_inc(st_ready, 1)

            def mask_unit(g):
                dve.wait_ge(e_ready, g + 1)
                V.scalar_tensor_tensor(out=wts[:, g % RING, :], in0=ps[0:128, g % NA, 0:HALF], scalar=0.0,
                                       in1=wts[:, g % RING, :], op0=ALU.is_ge, op1=ALU.mult).then_inc(w_ready, 1)

            def take_sum(k):
                h, s = k // 2, k % 2
                dve.wait_ge(out_done, CH * (k + 1))
                if s == 0:
                    dve.wait_ge(v2_mm, h + 1)
                V.tensor_tensor(half(kv[:, :], s), ps[0:128, ACC, 0:HALF], half(rz_row[:, h % 2, :], s), ALU.mult)\
                    .then_inc(kv_ready, 1)

            def attend(hh, u):
                s = s2[0:L, :].rearrange("p (b m) -> p b m", b=NB)
                if u == 3:
                    dve.wait_ge(s2_mm, hh + 1)
                    if hh == 1:
                        dve.wait_ge(y_stored, 16)
                    for k in range(2):
                        last = V.tensor_tensor(
                            s[:, 4 * k:4 * k + 4, :], ps[0:L, AT + k, 0:HALF].rearrange("p (b m) -> p b m", b=4),
                            causal[:, :].unsqueeze(1).to_broadcast([L, 4, L]), ALU.add)
                    last.then_inc(s2_add, 1)
                if u == 4:
                    dve.wait_ge(s2_add, hh + 1)
                    V.tensor_reduce(red2[:, 0, :], s, AX.X, ALU.max).then_inc(s2_red, 1)
                if u == 8:
                    dve.wait_ge(s2_exp, hh + 1)
                    V.tensor_reduce(red2[:, 1, :], s, AX.X, ALU.add).then_inc(s2_sum, 1)
                if u == 9:
                    dve.wait_ge(s2_sum, hh + 1)
                    V.reciprocal(red2[:, 1, :], red2[:, 1, :]).then_inc(s2_inv, 1)
                if u == 19:
                    dve.wait_ge(ffn_mm, hh + 1)
                    if hh == 1:
                        dve.wait_ge(h_moved, 1)
                    V.tensor_tensor(halves(h_sb[:, :]), pair(C), halves(h_sb[:, :]), ALU.add)\
                        .then_inc(ffn_added, 1)
                if u == 21 and hh == 0:
                    dve.wait_ge(y_mm, 1)
                    V.tensor_copy(h_sb[:, :], hf).then_inc(h_moved, 1)

            def run(kind):
                for hh, u, q, dense, front_on, ahead, behind in slots(kind):
                    n0 = first_tile(kind, hh)
                    g = 2 * q
                    if dense:
                        mask_unit(g)
                    if behind and hh <= H and g > 0 and g % CH == 0 and g <= H * UNITS:
                        take_sum(g // CH - 1)
                    if dense:
                        mask_unit(g + 1)
                    if ahead:
                        h = 0 if kind == "first" else hh + 1
                        if tile_at(u, 14) is not None:
                            low_part(n0 + tile_at(u, 14), h, tile_at(u, 14))
                        if tile_at(u, 12) is not None:
                            invert_sum(n0 + tile_at(u, 12))
                        for step in reversed(range(5)):
                            if tile_at(u, 5 + step) is not None:
                                top24(n0 + tile_at(u, 5 + step), step)
                        for step in (1, 2, 3):
                            if tile_at(u, step) is not None:
                                best16(n0 + tile_at(u, step), step)
                    if behind:
                        attend(hh, u)
                    if front_on:
                        front(q, kind)
                    if kind != "last" and hh == H - 1 and u == 30:
                        dve.wait_ge(ln_ready, 4)
                        if kind == "middle":
                            dve.wait_ge(q2_mm, H)
                        V.tensor_copy(xh[:, :], xf)
                if kind == "middle":
                    take_sum(2 * H - 1)
            run("first")
            dve.drain().then_inc(pass_end, 1)
            dve.wait_ge(pass_clear, 1)
            with dve.Fori(0, ITERS - 1) as it:
                run("middle")
                dve.drain().then_inc(pass_end, 1)
                dve.wait_ge(pass_clear, it + 2)
            run("last")


def kernel(x, cls_tok, L0_tok_W, L0_tok_b, L0_attn_qkv_w, L0_attn_qkv_b, L0_attn_proj_w, L0_attn_proj_b,
           L0_attn_logit_scale, L0_attn_mlp1_w, L0_attn_mlp1_b, L0_attn_mlp2_w, L0_attn_mlp2_b,
           L0_ffn_Wq_pk, L0_ffn_pk_keys, L0_ffn_Wq, L0_ffn_keys_table, L0_ffn_values_table, L0_ffn_Wo):
    import concourse.bacc as bacc
    from concourse.bass_utils import run_bass_kernel_spmd as run

    a = {k: np.asarray(v) for k, v in locals().items() if k not in ("bacc", "run")}
    f = {k: v.astype(np.float32) for k, v in shape_constants().items()}
    col = lambda v: v.reshape(-1, 1)
    w_tok = np.zeros((4, 4, GRID, GRID, C), np.float32)
    for m, (row, column) in enumerate([(0, 0), (1, 0), (0, 1), (1, 1), (3, 2), (2, 3), (3, 3)]):
        for j in range(GRID):
            w_tok[row, column, j, j] = a["L0_tok_W"][m]
    qkv_w, qkv_b = a["L0_attn_qkv_w"], a["L0_attn_qkv_b"]
    rows = np.concatenate([a["L0_ffn_keys_table"], a["L0_ffn_values_table"]], axis=1)
    f.update({
        "x": np.roll(a["x"], -NB, axis=0),
        "w_tok": w_tok.reshape(128, -1),
        "tok_b": col(a["L0_tok_b"]), "cls_tok": col(a["cls_tok"]),
        "w_qk": qkv_w[0:2 * C].T, "b_qk": col(qkv_b[0:2 * C]),
        "w_v": qkv_w[2 * C:].T, "b_v": np.broadcast_to(qkv_b[2 * C:], (L, C)),
        "w_proj": a["L0_attn_proj_w"].T, "b_proj": col(a["L0_attn_proj_b"]),
        "q_scale": col(np.repeat(a["L0_attn_logit_scale"], HD)),
        "mlp1": np.concatenate([a["L0_attn_mlp1_w"].T, a["L0_attn_mlp1_b"][None]]),
        "mlp2": np.concatenate([a["L0_attn_mlp2_w"].T, a["L0_attn_mlp2_b"][None]]),
        "w_q2": a["L0_ffn_Wq"],
        "w_o2": a["L0_ffn_Wo"].reshape(H, C, C).transpose(1, 0, 2).reshape(C, H * C),
        "pk_q": a["L0_ffn_Wq_pk"].reshape(C, 2, H, DK).transpose(3, 2, 1, 0).reshape(DK, 2 * H, C),
        "pk_k": a["L0_ffn_pk_keys"].transpose(3, 2, 0, 1).reshape(DK, 2 * H, NK),
        "table": rows.reshape(H, CH, 128, 128).transpose(2, 0, 1, 3).reshape(128, H, CH * 128),
    })
    nc = bacc.Bacc("TRN2", target_bir_lowering=False, num_devices=1)
    arrays, dram = {}, {}
    for name, v in f.items():
        v = np.ascontiguousarray(v)
        arrays[f"in_{name}"] = v
        dram[name] = nc.dram_tensor(f"in_{name}", v.shape, mybir.dt.from_np(v.dtype), kind="ExternalInput").ap()
    dram["out"] = nc.dram_tensor("out", (B, L, C), F32, kind="ExternalOutput").ap()
    build(nc, dram)
    r = run(nc, [arrays], core_ids=[0])
    return r.results[0]["out"]
```
